# Optimizing a Trainium2 kernel written in Bass

```python
import numpy as np
import jax
import jax.numpy as jnp

def _softmax(x, axis=-1):
    return jax.nn.softmax(x, axis=axis)

def _gelu(x):
    return jax.nn.gelu(x, approximate=True)

def _silu(x):
    return jax.nn.silu(x)

def _sigmoid(x):
    return jax.nn.sigmoid(x)

def _layernorm(x, axis=-1, eps=1e-05):
    m = jnp.mean(x, axis=axis, keepdims=True)
    v = jnp.var(x, axis=axis, keepdims=True)
    return (x - m) / jnp.sqrt(v + eps)

def _scatter_add(tgt, idx, src, axis=0):
    return tgt.at[idx].add(src)

def _segment_sum(src, seg, n):
    return jax.ops.segment_sum(src, seg, n)
kernel_name = 'mk_audio_tower_d2_tok_aud1d768_r4_a55e33'

def setup_inputs(seed: int=0):
    np.random.seed(seed)
    _w = jnp.asarray

    def _rec_inputs():
        import jax
        import jax.numpy as jnp
        _rk = jax.random.key(seed)
        x = -6.41493e-05 + 1.00002 * jax.random.normal(jax.random.fold_in(_rk, 1), (32, 40000), jnp.float32)
        return x
    x = _rec_inputs()

    def _L0_tok_setup():
        import jax, jax.numpy as jnp
        import numpy as np
        import math
        SR = 4000
        FRAME_LEN = 100
        FRAME_STEP = 160
        N_FILTERS = 40
        N_MFCC = 13
        EMBED = 192
        BATCH = 64
        AUDIO_LEN = 40000
        N_FFT_BINS = FRAME_LEN // 2 + 1

        def _mel_filterbank():
            low_mel = 2595.0 * math.log10(1.0 + 0.0 / 700.0)
            high_mel = 2595.0 * math.log10(1.0 + SR // 2 / 700.0)
            mel_points = np.linspace(low_mel, high_mel, N_FILTERS + 2)
            hz_points = 700.0 * (10.0 ** (mel_points / 2595.0) - 1.0)
            bin_points = np.floor((FRAME_LEN + 1) * hz_points / SR)
            filt = np.zeros((N_FILTERS, N_FFT_BINS), dtype=np.float32)
            for i in range(1, N_FILTERS + 1):
                l, c, r = (bin_points[i - 1], bin_points[i], bin_points[i + 1])
                for j in range(int(l), int(c)):
                    filt[i - 1, j] = (j - l) / (c - l)
                for j in range(int(c), int(r)):
                    filt[i - 1, j] = (r - j) / (r - c)
            return jnp.asarray(filt)

        def _dct_matrix():
            k = np.arange(N_MFCC)[:, None]
            j = np.arange(N_FILTERS)[None, :]
            m = np.cos(np.pi * k * (2 * j + 1) / (2 * N_FILTERS)) * math.sqrt(2.0 / N_FILTERS)
            return jnp.asarray(m.astype(np.float32))
        key = jax.random.key(seed)
        kx, kw = jax.random.split(key)
        x = jax.random.normal(kx, (BATCH, AUDIO_LEN), dtype=jnp.float32)
        bound = 1.0 / math.sqrt(N_MFCC)
        w_proj = jax.random.uniform(kw, (N_MFCC, EMBED), minval=-bound, maxval=bound, dtype=jnp.float32)
        b_proj = jnp.zeros((EMBED,), dtype=jnp.float32)
        return {'x': x, 'mel_filters': _mel_filterbank(), 'dct': _dct_matrix(), 'w_proj': w_proj, 'b_proj': b_proj}
    _L0_tok_all = _L0_tok_setup()
    _L0_tok_in = {k: v for k, v in _L0_tok_all.items() if k in ('mel_filters', 'dct', 'w_proj', 'b_proj')}
    del _L0_tok_all

    def _L0_attn_setup():
        import jax, jax.numpy as jnp
        import numpy as np
        B, N, C = (64, 80, 192)
        NUM_HEADS = 12
        LENS_Z = 64
        SCALE = (C // NUM_HEADS) ** (-0.5)
        key = jax.random.key(seed)
        k1, k2, k3 = jax.random.split(key, 3)
        x = jax.random.normal(k1, (B, N, C), dtype=jnp.float32)
        proj_w = jax.random.normal(k2, (C, C), dtype=jnp.float32) * 0.02
        proj_b = jax.random.normal(k3, (C,), dtype=jnp.float32) * 0.02
        return {'x': x, 'proj_w': proj_w, 'proj_b': proj_b}
    _L0_attn_all = _L0_attn_setup()
    _L0_attn_in = {k: v for k, v in _L0_attn_all.items() if k in ('proj_w', 'proj_b')}
    del _L0_attn_all

    def _L0_ffn_setup():
        import jax, jax.numpy as jnp
        import numpy as np
        B, S, H = (4, 2048, 192)
        E, K = (8, 2)
        key = jax.random.key(seed)
        ks = jax.random.split(key, 5)
        scale = 1.0 / np.sqrt(H)
        x = jax.random.normal(ks[0], (B, S, H), dtype=jnp.float32)
        router_w = jax.random.uniform(ks[1], (E, H), jnp.float32, -scale, scale)
        router_b = jax.random.uniform(ks[2], (E,), jnp.float32, -scale, scale)
        expert_w = jax.random.uniform(ks[3], (E, H, H), jnp.float32, -scale, scale)
        expert_b = jax.random.uniform(ks[4], (E, H), jnp.float32, -scale, scale)
        return {'x': x, 'router_w': router_w, 'router_b': router_b, 'expert_w': expert_w, 'expert_b': expert_b}
    _L0_ffn_all = _L0_ffn_setup()
    _L0_ffn_in = {k: v for k, v in _L0_ffn_all.items() if k in ('router_w', 'router_b', 'expert_w', 'expert_b')}
    del _L0_ffn_all

    def _L1_attn_setup():
        import jax, jax.numpy as jnp
        import numpy as np
        B, C, D = (8, 512, 192)
        EPS = 1e-05
        key = jax.random.key(seed)
        kx, kk, kq, kv = jax.random.split(key, 4)
        x = jax.random.normal(kx, (B, C, D), dtype=jnp.float32)
        s = 1.0 / np.sqrt(D)
        Wk = jax.random.uniform(kk, (D, D), dtype=jnp.float32, minval=-s, maxval=s)
        Wq = jax.random.uniform(kq, (D, D), dtype=jnp.float32, minval=-s, maxval=s)
        Wv = jax.random.uniform(kv, (D, D), dtype=jnp.float32, minval=-s, maxval=s)
        return {'x': x, 'Wk': Wk, 'Wq': Wq, 'Wv': Wv}
    _L1_attn_all = _L1_attn_setup()
    _L1_attn_in = {k: v for k, v in _L1_attn_all.items() if k in ('Wk', 'Wq', 'Wv')}
    del _L1_attn_all

    def _L1_ffn_setup():
        import jax, jax.numpy as jnp
        import numpy as np
        H = 192
        R = 64
        E = 8
        B, S = (8, 512)
        key = jax.random.key(seed)
        ks = jax.random.split(key, 10)
        s_in = 1.0 / np.sqrt(H)
        s_r = 1.0 / np.sqrt(R)
        return {'x': jax.random.normal(ks[0], (B, S, H), dtype=jnp.float32), 'enc_w': jax.random.uniform(ks[1], (H, R), jnp.float32, -s_in, s_in), 'enc_b': jax.random.uniform(ks[2], (R,), jnp.float32, -s_in, s_in), 'sw_w': jax.random.uniform(ks[3], (R, E), jnp.float32, -s_r, s_r), 'sw_b': jax.random.uniform(ks[4], (E,), jnp.float32, -s_r, s_r), 'w1': jax.random.uniform(ks[5], (E, H, R), jnp.float32, -s_in, s_in), 'b1': jax.random.uniform(ks[6], (E, R), jnp.float32, -s_in, s_in), 'w2': jax.random.uniform(ks[7], (E, R, H), jnp.float32, -s_r, s_r), 'b2': jax.random.uniform(ks[8], (E, H), jnp.float32, -s_r, s_r)}
    _L1_ffn_all = _L1_ffn_setup()
    _L1_ffn_in = {k: v for k, v in _L1_ffn_all.items() if k in ('enc_w', 'enc_b', 'sw_w', 'sw_b', 'w1', 'b1', 'w2', 'b2')}
    del _L1_ffn_all
    return {'x': x, 'L0_tok_mel_filters': _L0_tok_in['mel_filters'], 'L0_tok_dct': _L0_tok_in['dct'], 'L0_tok_w_proj': _L0_tok_in['w_proj'], 'L0_tok_b_proj': _L0_tok_in['b_proj'], 'L0_attn_proj_w': _L0_attn_in['proj_w'], 'L0_attn_proj_b': _L0_attn_in['proj_b'], 'L0_ffn_router_w': _L0_ffn_in['router_w'], 'L0_ffn_router_b': _L0_ffn_in['router_b'], 'L0_ffn_expert_w': _L0_ffn_in['expert_w'], 'L0_ffn_expert_b': _L0_ffn_in['expert_b'], 'L1_attn_Wk': _L1_attn_in['Wk'], 'L1_attn_Wq': _L1_attn_in['Wq'], 'L1_attn_Wv': _L1_attn_in['Wv'], 'L1_ffn_enc_w': _L1_ffn_in['enc_w'], 'L1_ffn_enc_b': _L1_ffn_in['enc_b'], 'L1_ffn_sw_w': _L1_ffn_in['sw_w'], 'L1_ffn_sw_b': _L1_ffn_in['sw_b'], 'L1_ffn_w1': _L1_ffn_in['w1'], 'L1_ffn_b1': _L1_ffn_in['b1'], 'L1_ffn_w2': _L1_ffn_in['w2'], 'L1_ffn_b2': _L1_ffn_in['b2']}

def reference(x, L0_tok_mel_filters, L0_tok_dct, L0_tok_w_proj, L0_tok_b_proj, L0_attn_proj_w, L0_attn_proj_b, L0_ffn_router_w, L0_ffn_router_b, L0_ffn_expert_w, L0_ffn_expert_b, L1_attn_Wk, L1_attn_Wq, L1_attn_Wv, L1_ffn_enc_w, L1_ffn_enc_b, L1_ffn_sw_w, L1_ffn_sw_b, L1_ffn_w1, L1_ffn_b1, L1_ffn_w2, L1_ffn_b2):
    import jax
    import jax.numpy as jnp

    def _L0_tok_ref(x, mel_filters, dct, w_proj, b_proj):
        import jax, jax.numpy as jnp
        import numpy as np
        import math
        SR = 4000
        FRAME_LEN = 100
        FRAME_STEP = 160
        N_FILTERS = 40
        N_MFCC = 13
        EMBED = 192
        BATCH = 64
        AUDIO_LEN = 40000
        N_FFT_BINS = FRAME_LEN // 2 + 1

        def _mel_filterbank():
            low_mel = 2595.0 * math.log10(1.0 + 0.0 / 700.0)
            high_mel = 2595.0 * math.log10(1.0 + SR // 2 / 700.0)
            mel_points = np.linspace(low_mel, high_mel, N_FILTERS + 2)
            hz_points = 700.0 * (10.0 ** (mel_points / 2595.0) - 1.0)
            bin_points = np.floor((FRAME_LEN + 1) * hz_points / SR)
            filt = np.zeros((N_FILTERS, N_FFT_BINS), dtype=np.float32)
            for i in range(1, N_FILTERS + 1):
                l, c, r = (bin_points[i - 1], bin_points[i], bin_points[i + 1])
                for j in range(int(l), int(c)):
                    filt[i - 1, j] = (j - l) / (c - l)
                for j in range(int(c), int(r)):
                    filt[i - 1, j] = (r - j) / (r - c)
            return jnp.asarray(filt)

        def _dct_matrix():
            k = np.arange(N_MFCC)[:, None]
            j = np.arange(N_FILTERS)[None, :]
            m = np.cos(np.pi * k * (2 * j + 1) / (2 * N_FILTERS)) * math.sqrt(2.0 / N_FILTERS)
            return jnp.asarray(m.astype(np.float32))
        B, T = x.shape
        n_frames = 1 + (T - FRAME_LEN) // FRAME_STEP
        idx = jnp.arange(n_frames)[:, None] * FRAME_STEP + jnp.arange(FRAME_LEN)[None, :]
        frames = x[:, idx]
        window = 0.54 - 0.46 * jnp.cos(2.0 * jnp.pi * jnp.arange(FRAME_LEN, dtype=jnp.float32) / (FRAME_LEN - 1))
        windowed = frames * window
        fft = jnp.fft.rfft(windowed, axis=-1)
        power = fft.real ** 2 + fft.imag ** 2
        mel_energies = jnp.einsum('bnf,mf->bnm', power, mel_filters)
        log_energies = jnp.log(mel_energies + 1e-06)
        mfcc = jnp.einsum('bnm,km->bnk', log_energies, dct)
        out = mfcc @ w_proj + b_proj
        return out

    def _L0_attn_ref(x, proj_w, proj_b):
        import jax, jax.numpy as jnp
        import numpy as np
        B, N, C = (64, 80, 192)
        NUM_HEADS = 12
        LENS_Z = 64
        SCALE = (C // NUM_HEADS) ** (-0.5)
        q = x[:, :LENS_Z]
        k = x[:, LENS_Z:]
        v = k
        attn = jnp.einsum('bqc,bkc->bqk', q, k) * SCALE
        attn = jax.nn.softmax(attn, axis=-1)
        out = jnp.einsum('bqk,bkc->bqc', attn, v)
        out = jnp.transpose(out, (0, 2, 1)).reshape(out.shape[0], -1, C)
        out = out @ proj_w.T + proj_b
        return jnp.concatenate([out, k], axis=1)

    def _L0_ffn_ref(x, router_w, router_b, expert_w, expert_b):
        import jax, jax.numpy as jnp
        import numpy as np
        B, S, H = (4, 2048, 192)
        E, K = (8, 2)
        scores = jnp.einsum('bsh,eh->bse', x, router_w) + router_b
        probs = jax.nn.softmax(scores, axis=-1)
        top_probs, expert_ids = jax.lax.top_k(probs, K)
        y = jnp.einsum('bsh,edh->bsed', x, expert_w) + expert_b
        out_k = jnp.take_along_axis(y, expert_ids[..., None], axis=2)
        w = top_probs / (jnp.sum(top_probs, axis=-1, keepdims=True) + 1e-09)
        out = jnp.einsum('bsk,bskh->bsh', w, out_k)
        return out

    def _L1_attn_ref(x, Wk, Wq, Wv):
        import jax, jax.numpy as jnp
        import numpy as np
        B, C, D = (8, 512, 192)
        EPS = 1e-05
        mean = jnp.mean(x, axis=(-2, -1), keepdims=True)
        var = jnp.mean(jnp.square(x - mean), axis=(-2, -1), keepdims=True)
        xn = (x - mean) * jax.lax.rsqrt(var + EPS)
        keys = jnp.einsum('bcd,od->bco', xn, Wk)
        queries = jnp.einsum('bcd,od->bco', xn, Wq)
        values = jnp.einsum('bcd,od->bco', xn, Wv)
        att = jax.nn.softmax(jnp.einsum('bid,bjd->bij', queries, keys), axis=-1)
        return jnp.einsum('bjd,bij->bid', values, att)

    def _L1_ffn_ref(x, enc_w, enc_b, sw_w, sw_b, w1, b1, w2, b2):
        import jax, jax.numpy as jnp
        import numpy as np
        H = 192
        R = 64
        E = 8
        B, S = (8, 512)
        b, s, d = x.shape
        xt = x.reshape(-1, d)
        x_enc = xt @ enc_w + enc_b
        route_prob = jax.nn.softmax(x_enc @ sw_w + sw_b, axis=-1)
        route_prob_max = jnp.max(route_prob, axis=-1)
        routes = jnp.argmax(route_prob, axis=-1)
        onehot = jax.nn.one_hot(routes, E, dtype=xt.dtype)
        h = jnp.einsum('td,edr->ter', xt, w1) + b1[None]
        h = jax.nn.gelu(h, approximate=False)
        h = h * onehot[..., None]
        out = jnp.einsum('ter,erd->td', h, w2) + onehot @ b2
        out = out * route_prob_max[:, None]
        return out.reshape(b, s, d)
    h = _L0_tok_ref(x, L0_tok_mel_filters, L0_tok_dct, L0_tok_w_proj, L0_tok_b_proj)
    h = h + _L0_attn_ref(_layernorm(h, axis=-1), L0_attn_proj_w, L0_attn_proj_b)
    h = h + _L0_ffn_ref(_layernorm(h, axis=-1), L0_ffn_router_w, L0_ffn_router_b, L0_ffn_expert_w, L0_ffn_expert_b)
    h = h + _L1_attn_ref(_layernorm(h, axis=-1), L1_attn_Wk, L1_attn_Wq, L1_attn_Wv)
    h = h + _L1_ffn_ref(_layernorm(h, axis=-1), L1_ffn_enc_w, L1_ffn_enc_b, L1_ffn_sw_w, L1_ffn_sw_b, L1_ffn_w1, L1_ffn_b1, L1_ffn_w2, L1_ffn_b2)
    return h

_drawn_inputs = setup_inputs


def setup_inputs(seed=0):
    import zlib

    import numpy as np

    out = dict(_drawn_inputs(seed))
    spreads = {'L0_tok_b_proj': (0.0, 0.322)}
    factors = {'L0_attn_proj_b': 8.0,
     'L0_ffn_router_b': 37.959,
     'L0_ffn_expert_b': 6.715,
     'L1_attn_Wk': 5.255,
     'L1_attn_Wq': 4.759,
     'L1_ffn_enc_w': 7.109,
     'L1_ffn_enc_b': 8.0,
     'L1_ffn_sw_w': 6.608,
     'L1_ffn_sw_b': 8.0,
     'L1_ffn_w1': 8.0,
     'L1_ffn_b1': 8.0,
     'L1_ffn_w2': 7.984,
     'L1_ffn_b2': 8.0}
    for name, (base, spread) in spreads.items():
        noise = np.random.default_rng([zlib.crc32(name.encode()), seed]).standard_normal(out[name].shape)
        drawn = base * np.exp(spread * noise) if base else spread * noise
        out[name] = jnp.asarray(drawn.astype(out[name].dtype))
    for name, factor in factors.items():
        out[name] = (out[name] * factor).astype(out[name].dtype)
    return out
```

```python
from contextlib import ExitStack

import concourse.bass as bass
from concourse import mybir

ALU = mybir.AluOpType
ACT = mybir.ActivationFunctionType
F32 = mybir.dt.float32
BF16 = mybir.dt.bfloat16
U32 = mybir.dt.uint32
AX_X = mybir.AxisListType.X

CLIPS, AUDIO = 32, 40000
FRAME, HOP = 100, 160
TOKENS = 1 + (AUDIO - FRAME) // HOP
T = TOKENS // 2
BINS = FRAME // 2 + 1
MEL, MFCC = 40, 13
C = 192
CH = C // 2
QUERIES = 64
EXPERTS = 8
HID = 64
EPS = 1e-5
PAIR = 2 * C

STAGES = {"A": 0, "B": 1, "C": 2, "X": 3, "D": 4, "E": 5, "store": 6}
LAST = STAGES["store"]
FIRST_LOOPED = 8
END_LOOPED = CLIPS


def tower(nc, x, dft, ident, iota, expert_rows, mel_w, dct_w, embed_w, attn_w, attn_b,
          router_w, expert_w, wq, wk, wv, enc_w, switch_w, w1, w2, b2, out):
    frames = x.rearrange("b (t p n) -> b p t n", t=2, n=HOP)
    out_tokens = out.rearrange("b (t p) c -> b p t c", t=2)

    with ExitStack() as ctx:
        def sb(name, shape, dt=F32):
            return ctx.enter_context(nc.sbuf_tensor(name, shape, dt))

        def ps(name, shape, dt=F32):
            return ctx.enter_context(nc.psum_tensor(name, shape, dt))

        def sem(name):
            return ctx.enter_context(nc.semaphore(name))

        dft_sb = sb("dft_sb", [FRAME, 2 * BINS])
        ident_sb = sb("ident_sb", [128, 128])
        iota_sb = sb("iota_sb", [128, EXPERTS])
        rows_f = sb("rows_f", [EXPERTS, EXPERTS * HID])
        rows_b = sb("rows_b", [EXPERTS, EXPERTS * HID], BF16)
        mel_sb = sb("mel_sb", [2 * BINS, MEL])
        dct_sb = sb("dct_sb", [MFCC + 1, MEL + 1])
        embed_in = sb("embed_in", [MFCC + 1, C])
        embed_sb = sb("embed_sb", [MEL + 1, C])
        attn_sb = sb("attn_sb", [QUERIES + 1, 3, C])
        router_sb = sb("router_sb", [CH + 1, 2, EXPERTS])
        expert_sb = sb("expert_sb", [CH + 1, 2, EXPERTS * C])
        wq_sb = sb("wq_sb", [CH, 2, C])
        wk_sb = sb("wk_sb", [CH, 2, C])
        qk_sb = sb("qk_sb", [CH, 2, C])
        wv_sb = sb("wv_sb", [CH, 2, C])
        enc_sb = sb("enc_sb", [HID + 1, C + 1])
        switch_in = sb("switch_in", [HID + 1, EXPERTS])
        switch_sb = sb("switch_sb", [CH + 1, 2, EXPERTS])
        w1_sb = sb("w1_sb", [CH + 1, 2, EXPERTS * HID])
        w2_sb = sb("w2_sb", [128, 4, C])
        b2_sb = sb("b2_sb", [EXPERTS, C])
        mean_w = sb("mean_w", [T, 128])
        log_eps = sb("log_eps", [128, 1])
        minus_half = sb("minus_half", [128, 2])

        frame_sb = [sb(f"frame_sb{i}", [T, 2, FRAME]) for i in range(2)]
        frame_t = sb("frame_t", [FRAME, TOKENS])
        power = sb("power", [2 * BINS, TOKENS])
        log_mel = sb("log_mel", [MEL + 1, TOKENS])
        h0 = [sb(f"h0_{i}", [T, 2, C]) for i in range(2)]
        stats = [sb(f"stats{k}", [T, 2, 6]) for k in range(4)]
        moments = [sb(f"moments{k}", [T, 2, 2]) for k in range(4)]
        var_eps = [sb(f"var_eps{k}", [T, 2]) for k in range(4)]
        rdev = [sb(f"rdev{k}", [T, 2]) for k in range(4)]
        y0 = [sb(f"y0_{i}", [T, 2, C + 1]) for i in range(2)]
        y0_t = sb("y0_t", [CH, 2, TOKENS])
        probs_b = sb("probs_b", [T, 2, QUERIES])
        rsum_b = sb("rsum_b", [QUERIES, 1])
        mix_b = sb("mix_b", [QUERIES + 1, C])
        h1 = [sb(f"h1_{i}", [T, 2, C]) for i in range(2)]
        y1 = sb("y1", [T, 2, C])
        y1_t = [sb(f"y1_t{i}", [CH + 1, 2, TOKENS]) for i in range(2)]
        top = sb("top", [T, 2, 8])
        top_at = sb("top_at", [T, 2, 8], U32)
        neg_top = sb("neg_top", [T, 2])
        top_exp = sb("top_exp", [T, 2, 8])
        exp_sum = sb("exp_sum", [T, 2])
        denom = sb("denom", [T, 2])
        denom1 = sb("denom1", [T, 2])
        rdenom = sb("rdenom", [T, 2])
        pick_w = sb("pick_w", [T, 2, 2])
        pick_hot = sb("pick_hot", [T, 2, 2, EXPERTS])
        pick_mix = sb("pick_mix", [T, 2, 2, EXPERTS])
        mix_w = [sb(f"mix_w{i}", [T, 2, EXPERTS]) for i in range(2)]
        h2 = [sb(f"h2_{i}", [T, 2, C]) for i in range(2)]
        shift2 = sb("shift2", [T, 2])
        y2 = sb("y2", [T, 2, C])
        y2_sq = sb("y2_sq", [T, 2, C])
        clip_sums = sb("clip_sums", [T, 2, 2])
        clip_moments = sb("clip_moments", [128, 2])
        mean_sq = sb("mean_sq", [128, 1])
        clip_var = sb("clip_var", [128, 1])
        clip_var_eps = sb("clip_var_eps", [128, 1])
        clip_rdev = sb("clip_rdev", [128, 1])
        xn_t = sb("xn_t", [CH, 2, TOKENS])
        qk_t = sb("qk_t", [CH, 2, TOKENS])
        values = sb("values", [T, 2, C])
        neg_max = sb("neg_max", [T, 2])
        probs_d = sb("probs_d", [T, 2, TOKENS])
        probs_t = sb("probs_t", [T, 2, TOKENS])
        sum_d = sb("sum_d", [T, 2])
        rsum_d = sb("rsum_d", [T, 2])
        h3 = [sb(f"h3_{i}", [T, 2, C]) for i in range(2)]
        y3 = sb("y3", [T, 2, C])
        y3_t = sb("y3_t", [CH + 1, 2, TOKENS])
        best = sb("best", [T, 2, 8])
        best_at = sb("best_at", [T, 2, 8], U32)
        neg_best = sb("neg_best", [T, 2])
        route_exp = sb("route_exp", [T, 2, 8])
        route_sum = sb("route_sum", [T, 2])
        route_prob = sb("route_prob", [T, 2])
        hot = sb("hot", [T, 2, EXPERTS])
        hot_t = sb("hot_t", [EXPERTS, TOKENS])
        hot_tb = sb("hot_tb", [EXPERTS, TOKENS], BF16)
        act_h = sb("act_h", [128, 4, TOKENS])
        act_m = sb("act_m", [128, 4, TOKENS])
        out_sb = [sb(f"out_sb{i}", [T, 2, C]) for i in range(2)]

        bank_a = ps("bank_a", [128, 512])
        bank_b = ps("bank_b", [128, 512])
        bank_c = ps("bank_c", [128, 512])
        bank_d = ps("bank_d", [128, 512])
        bank_d2 = ps("bank_d2", [128, 512])
        bank_e = ps("bank_e", [128, 512])
        bank_x = [ps(f"bank_x{i}", [128, 512]) for i in range(2)]

        def halves(bank, rows, n):
            return bank[0:rows, 0:2 * n].rearrange("p (t n) -> p t n", t=2)

        s_load = sem("s_load")
        s_ones = sem("s_ones")
        s_fold = sem("s_fold")
        s_folded = sem("s_folded")
        s_frames = [sem(f"s_frames{i}") for i in range(2)]
        s_stored = [sem(f"s_stored{i}") for i in range(2)]
        pe_frames, pe_dft, pe_mel, pe_embed = (sem(n) for n in ("pe_frames", "pe_dft", "pe_mel", "pe_embed"))
        pe_y0t, pe_scores_b, pe_mix_b, pe_proj_b = (sem(n) for n in ("pe_y0t", "pe_scores_b", "pe_mix_b", "pe_proj_b"))
        pe_y1t, pe_router, pe_expert = (sem(n) for n in ("pe_y1t", "pe_router", "pe_expert"))
        pe_clip, pe_y2t, pe_qk, pe_values, pe_scores_d, pe_probs_t, pe_mix_d = (
            sem(n) for n in ("pe_clip", "pe_y2t", "pe_qk", "pe_values", "pe_scores_d", "pe_probs_t", "pe_mix_d"))
        pe_y3t, pe_switch, pe_hot_t, pe_mask, pe_hidden, pe_out = (
            sem(n) for n in ("pe_y3t", "pe_switch", "pe_hot_t", "pe_mask", "pe_hidden", "pe_out"))
        ac_frame_t, ac_power, ac_log, ac_y0t, ac_probs_b, ac_y1t, ac_top_exp = (
            sem(n) for n in ("ac_frame_t", "ac_power", "ac_log", "ac_y0t", "ac_probs_b", "ac_y1t", "ac_top_exp"))
        ac_sums, ac_y2, ac_qk, ac_values, ac_probs_d, ac_y3t, ac_route_exp, ac_gelu = (
            sem(n) for n in ("ac_sums", "ac_y2", "ac_qk", "ac_values", "ac_probs_d", "ac_y3t", "ac_route_exp", "ac_gelu"))
        ve_h0, ve_y0, ve_mix_b, ve_h1, ve_y1, ve_top, ve_mix_w, ve_pair, ve_combined = (
            sem(n) for n in ("ve_h0", "ve_y0", "ve_mix_b", "ve_h1", "ve_y1", "ve_top", "ve_mix_w", "ve_pair", "ve_combined"))
        ve_clip_var, ve_xnt, ve_max_d, ve_probs_t, ve_h3, ve_y3, ve_best, ve_hot, ve_hot_t, ve_masked, ve_out = (
            sem(n) for n in ("ve_clip_var", "ve_xnt", "ve_max_d", "ve_probs_t", "ve_h3", "ve_y3", "ve_best", "ve_hot",
                             "ve_hot_t", "ve_masked", "ve_out"))
        ve_moments = [sem(f"ve_moments{k}") for k in range(4)]
        ve_own = sem("ve_own")
        po_rdev = [sem(f"po_rdev{k}") for k in range(4)]
        po_shift2, po_h1, po_h2, po_clip_rdev, po_own = (
            sem(n) for n in ("po_shift2", "po_h1", "po_h2", "po_clip_rdev", "po_own"))

        block = ctx.enter_context(nc.Block())

        def run(eng, step):
            def at(j):
                def clip(stage):
                    b = j - STAGES[stage]
                    return b if 0 <= b < CLIPS else None
                step(j, j % 2, clip)

            for j in range(FIRST_LOOPED):
                at(j)
            with eng.Fori(FIRST_LOOPED, END_LOOPED - 1, 2) as i:
                for par in range(2):
                    step(i + par, par, lambda stage, par=par: i + (par - STAGES[stage]))
            for j in range(END_LOOPED, CLIPS + LAST):
                at(j)

        def settled(eng):
            eng.nop(nofuse=True)

        def old(b, back):
            return not isinstance(b, int) or b >= back

        LOADS_SP = [
            (ident_sb[:, :], ident), (dft_sb[:, :], dft), (mel_sb[:, :], mel_w), (dct_sb[:, :], dct_w),
            (embed_in[:, :], embed_w), (iota_sb[:, :], iota), (rows_f[:, :], expert_rows),
            (attn_sb[0:QUERIES, :, :], attn_w.rearrange("(a q) o -> q a o", q=QUERIES)),
            (attn_sb[QUERIES:QUERIES + 1, 0, :], attn_b),
            (router_sb[:, 0, :], router_w[0:CH + 1, :]),
            (router_sb[:, 1, :], router_w[CH:C + 1, :]),
            (enc_sb[:, :], enc_w), (switch_in[:, :], switch_w), (b2_sb[:, :], b2),
            (expert_sb[0:CH, 0, :], expert_w[0:CH, :]),
            (expert_sb[:, 1, :], expert_w[CH:C + 1, :]),
            (wq_sb[:, :, :], wq.rearrange("(t p) n -> p t n", t=2)),
            (wk_sb[:, :, :], wk.rearrange("(t p) n -> p t n", t=2)),
            (wv_sb[:, :, :], wv.rearrange("(t p) n -> p t n", t=2)),
            (w1_sb[0:CH, 0, :], w1[0:CH, :]),
            (w1_sb[:, 1, :], w1[CH:C + 1, :]),
            (w2_sb[:, :, :], w2.rearrange("(t p) n -> p t n", t=4)),
        ]
        LOADED = 16 * len(LOADS_SP)

        @block.sync
        def _(sp):
            for dst, src in LOADS_SP:
                sp.dma_start(dst, src).then_inc(s_load, 16)

            def step(j, par, clip):
                a, e = clip("A"), clip("store")
                if a is not None:
                    if old(a, 2):
                        sp.wait_ge(pe_frames, a - 1)
                    src = frames[a] if isinstance(a, int) else frames[bass.ds(a, 1)].rearrange(
                        "a p t n -> (a p) t n")
                    sp.dma_start(frame_sb[par][:, :, :], src[:, :, 0:FRAME]).then_inc(s_frames[par], 16)
                if e is not None:
                    sp.wait_ge(ve_out, e + 1)
                    dst = out_tokens[e] if isinstance(e, int) else out_tokens[bass.ds(e, 1)].rearrange(
                        "a p t c -> (a p) t c")
                    ep = (par + STAGES["store"]) % 2
                    sp.dma_start(dst, out_sb[ep][:, :, :]).then_inc(s_stored[ep], 16)

            run(sp, step)
            for i in range(2):
                sp.wait_ge(s_stored[i], 16 * (CLIPS // 2))


        @block.gpsimd
        def _(pool):
            pool.memset(log_eps[:, :], 1e-6)
            pool.memset(minus_half[:, :], -0.5)
            pool.memset(mean_w[:, :], 1.0 / (TOKENS * C))
            pool.memset(log_mel[:, :], 1.0)
            pool.memset(mix_b[:, :], 1.0)
            pool.memset(probs_b[:, :, :], 0.0)
            pool.memset(y3_t[:, :, :], 1.0)
            for i in range(2):
                pool.memset(y1_t[i][:, :, :], 1.0)
                pool.memset(y0[i][:, :, :], 1.0)
            pool.memset(neg_top[:, :], 0.0).then_inc(s_ones, 1)
            pool.wait_ge(s_ones, 1)

            def layernorm(k, b):
                pool.wait_ge(ve_moments[k], b + 1)
                settled(pool)
                pool.tensor_scalar(var_eps[k][:, :], moments[k][:, :, 1], EPS, None,
                                   ALU.add).then_inc(po_own, 1)

            def power_minus_half(k):
                pool.tensor_tensor(rdev[k][:, :], var_eps[k][:, :], minus_half[0:T, :],
                                   ALU.pow).then_inc(po_rdev[k], 1)

            def step(j, par, clip):
                a, b, x_, d = clip("A"), clip("B"), clip("X"), clip("D")
                own = pool_own_before(clip, j)
                if x_ is not None:
                    xp = (par + STAGES["X"]) % 2
                    pool.wait_ge(ve_h1, x_ + 1)
                    pool.wait_ge(po_h1, x_ + 1)
                    if old(x_, 2):
                        pool.wait_ge(ve_h3, x_ - 1)
                    settled(pool)
                    pool.tensor_copy(h2[xp][:, :, :], h1[xp][:, :, :]).then_inc(po_h2, 1)
                if d is not None:
                    pool.wait_ge(ve_clip_var, d + 1)
                    settled(pool)
                    pool.tensor_scalar(clip_var_eps[:, :], clip_var[:, :], EPS, None,
                                       ALU.add).then_inc(po_own, 1)
                    own = own + 1
                    pool.wait_ge(po_own, own)
                    pool.tensor_tensor(clip_rdev[:, :], clip_var_eps[:, :], minus_half[:, 0:1],
                                       ALU.pow).then_inc(po_clip_rdev, 1)
                if b is not None:
                    bp = (par + STAGES["B"]) % 2
                    pool.wait_ge(ve_y0, b + 1)
                    if old(b, 2):
                        pool.wait_ge(po_h2, b - 1)
                        pool.wait_ge(ve_y1, b - 1)
                    pool.tensor_tensor(h1[bp][:, :, :], h0[bp][:, :, :], y0[bp][:, :, 0:C],
                                       ALU.add).then_inc(po_h1, 1)
                if a is not None:
                    layernorm(0, a)
                    own = own + 1
                    pool.wait_ge(po_own, own)
                    power_minus_half(0)
                if b is not None:
                    layernorm(1, b)
                    own = own + 1
                    pool.wait_ge(po_own, own)
                    power_minus_half(1)
                if d is not None:
                    layernorm(3, d)
                    own = own + 1
                    pool.wait_ge(po_own, own)
                    power_minus_half(3)
                if x_ is not None:
                    if old(x_, 1):
                        pool.wait_ge(ac_y2, x_)
                    layernorm(2, x_)
                    own = own + 1
                    pool.wait_ge(po_own, own)
                    power_minus_half(2)
                    pool.wait_ge(po_rdev[2], x_ + 1)
                    pool.tensor_tensor(shift2[:, :], moments[2][:, :, 0], rdev[2][:, :],
                                       ALU.mult).then_inc(po_own, 1)
                    own = own + 1
                    pool.wait_ge(po_own, own)
                    settled(pool)
                    pool.tensor_scalar(shift2[:, :], shift2[:, :], -1.0, None,
                                       ALU.mult).then_inc(po_shift2, 1)

            def pool_own_before(clip, j):
                counts = [("A", 1), ("B", 1), ("D", 2), ("X", 2)]
                if isinstance(j, int):
                    return sum(n * min(max(j - STAGES[s], 0), CLIPS) for s, n in counts)
                total = sum(n for _, n in counts)
                return j * total - sum(n * STAGES[s] for s, n in counts)

            run(pool, step)

        @block.scalar
        def _(act):
            act.wait_ge(s_load, LOADED)
            act.wait_ge(s_ones, 1)
            act.activation(rows_b[:, :], rows_f[:, :], ACT.Copy).then_inc(s_folded, 1)
            act.wait_ge(s_fold, 1)
            act.activation(embed_sb[:, :], bank_a[0:MEL + 1, 0:C], ACT.Copy).then_inc(s_folded, 1)
            act.activation(qk_sb[:, :, :], halves(bank_b, CH, C), ACT.Copy).then_inc(s_folded, 1)
            act.activation(switch_sb[:, :, :], halves(bank_c, CH + 1, EXPERTS), ACT.Copy).then_inc(s_folded, 1)

            def step(j, par, clip):
                a, b, c, x_, d, e = (clip(s) for s in "ABCXDE")
                if a is not None:
                    act.wait_ge(pe_frames, a + 1)
                    act.activation(frame_t[:, :], bank_a[0:FRAME, 0:TOKENS], ACT.Copy).then_inc(ac_frame_t, 1)
                if b is not None:
                    act.wait_ge(pe_y0t, b + 1)
                    act.activation(y0_t[:, :, :], halves(bank_b, CH, TOKENS), ACT.Copy).then_inc(ac_y0t, 1)
                if c is not None:
                    act.wait_ge(pe_y1t, c + 1)
                    if old(c, 2):
                        act.wait_ge(pe_expert, 8 * (c - 1))
                    cp = (par + STAGES["C"]) % 2
                    act.activation(y1_t[cp][0:CH, :, :], halves(bank_c, CH, TOKENS),
                                   ACT.Copy).then_inc(ac_y1t, 1)
                if e is not None:
                    act.wait_ge(pe_y3t, e + 1)
                    act.activation(y3_t[0:CH, :, :], halves(bank_e, CH, TOKENS), ACT.Copy).then_inc(ac_y3t, 1)
                if a is not None:
                    act.wait_ge(pe_dft, a + 1)
                    act.activation(power[:, :], bank_a[0:2 * BINS, 0:TOKENS], ACT.Square).then_inc(ac_power, 1)
                if a is not None:
                    act.wait_ge(pe_mel, a + 1)
                    act.activation(log_mel[0:MEL, :], bank_a[0:MEL, 0:TOKENS], ACT.Ln,
                                   bias=log_eps[0:MEL, :]).then_inc(ac_log, 1)
                if b is not None:
                    act.wait_ge(pe_scores_b, b + 1)
                    act.activation(probs_b[QUERIES:T, 0, :], bank_b[QUERIES:T, 0:QUERIES], ACT.Exp,
                                   scale=0.25)
                    act.activation(probs_b[:, 1, :], bank_b[0:T, QUERIES:2 * QUERIES], ACT.Exp,
                                   scale=0.25).then_inc(ac_probs_b, 1)
                if c is not None:
                    act.wait_ge(ve_top, c + 1)
                    for t in range(2):
                        act.activation(top_exp[:, t, :], top[:, t, :], ACT.Exp, bias=neg_top[:, t:t + 1],
                                       accum_out=exp_sum[:, t:t + 1]).then_inc(ac_top_exp, 1)
                if e is not None:
                    act.wait_ge(ve_best, e + 1)
                    for t in range(2):
                        act.activation(route_exp[:, t, :], best[:, t, :], ACT.Exp, bias=neg_best[:, t:t + 1],
                                       accum_out=route_sum[:, t:t + 1]).then_inc(ac_route_exp, 1)
                if d is not None:
                    act.wait_ge(pe_qk, d + 1)
                    act.activation(qk_t[:, :, :], halves(bank_d, CH, TOKENS), ACT.Copy).then_inc(ac_qk, 1)
                    act.wait_ge(pe_values, d + 1)
                    act.activation(values[:, :, :], halves(bank_d2, T, C), ACT.Copy).then_inc(ac_values, 1)
                    act.wait_ge(ve_max_d, d + 1)
                    if old(d, 1):
                        act.wait_ge(ve_h3, d)
                    for t in range(2):
                        act.activation(probs_d[:, t, :], bank_d[0:T, t * TOKENS:(t + 1) * TOKENS], ACT.Exp,
                                       bias=neg_max[:, t:t + 1],
                                       accum_out=sum_d[:, t:t + 1]).then_inc(ac_probs_d, 1)
                if e is not None:
                    for g in range(2):
                        act.wait_ge(pe_hidden, 2 * e + g + 1)
                        act.activation(act_h[:, 2 * g:2 * g + 2, :], halves(bank_c, 128, TOKENS),
                                       ACT.Gelu).then_inc(ac_gelu, 1)
                if x_ is not None:
                    xp = (par + STAGES["X"]) % 2
                    act.wait_ge(ve_combined, 8 * x_ + 8)
                    act.wait_ge(po_shift2, x_ + 1)
                    if old(x_, 1):
                        act.wait_ge(pe_y2t, x_)
                    for t in range(2):
                        act.activation(y2[:, t, :], h2[xp][:, t, :], ACT.Identity, scale=rdev[2][:, t:t + 1],
                                       bias=shift2[:, t:t + 1], accum_out=clip_sums[:, t, 0:1])
                        last = act.activation(y2_sq[:, t, :], h2[xp][:, t, :], ACT.Square,
                                              scale=rdev[2][:, t:t + 1], bias=shift2[:, t:t + 1],
                                              accum_out=clip_sums[:, t, 1:2])
                    last.then_inc(ac_y2, 1)

            run(act, step)

        @block.tensor
        def _(pe):
            pe.wait_ge(s_load, LOADED)
            pe.wait_ge(s_ones, 1)
            pe.matmul(bank_a[0:MEL + 1, 0:C], dct_sb[:, :], embed_in[:, :], start=True, stop=True)
            for m in range(2):
                for k in range(2):
                    pe.matmul(halves(bank_b, CH, C)[:, m, :], wq_sb[:, k, m * CH:(m + 1) * CH], wk_sb[:, k, :],
                              start=(k == 0), stop=(k == 1))
            pe.matmul(bank_c[0:CH + 1, 0:EXPERTS], enc_sb[:, 0:CH + 1], switch_in[:, :], start=True, stop=True)
            pe.matmul(bank_c[0:CH + 1, EXPERTS:2 * EXPERTS], enc_sb[:, CH:C + 1], switch_in[:, :],
                      start=True, stop=True).then_inc(s_fold, 1)
            pe.wait_ge(s_folded, 4)

            def transposes(bank, src):
                for k in range(2):
                    for t in range(2):
                        last = pe.transpose(bank[0:CH, k * TOKENS + t * T:k * TOKENS + (t + 1) * T],
                                            src[:, t, k * CH:(k + 1) * CH], ident_sb[0:T, 0:T])
                return last

            def rows(half):
                return CH + half

            def experts(x_, xp, g):
                t, pair = g // 4, g % 4
                if g >= 2 or old(x_, 1):
                    pe.wait_ge(ve_combined, 8 * x_ + g - 1)
                for k in range(2):
                    last = pe.matmul(bank_x[g % 2][0:T, 0:PAIR], y1_t[xp][0:rows(k), k, t * T:(t + 1) * T],
                                     expert_sb[0:rows(k), k, pair * PAIR:(pair + 1) * PAIR],
                                     start=(k == 0), stop=(k == 1))
                last.then_inc(pe_expert, 1)

            def step(j, par, clip):
                a, b, c, x_, d, e = (clip(s) for s in "ABCXDE")
                bp, xp, ep = ((par + STAGES[s]) % 2 for s in "BXE")
                cp = par
                if a is not None:
                    half_count = (a // 2 + 1) * 16 if isinstance(a, int) else (a + (2 - par)) * 8
                    pe.wait_ge(s_frames[par], half_count)
                    if old(a, 1):
                        pe.wait_ge(ve_h0, a)
                    for t in range(2):
                        last = pe.transpose(bank_a[0:FRAME, t * T:(t + 1) * T], frame_sb[par][:, t, :],
                                            ident_sb[0:T, 0:T])
                    last.then_inc(pe_frames, 1)
                if b is not None:
                    pe.wait_ge(ve_y0, b + 1)
                    if old(b, 1):
                        pe.wait_ge(ve_h1, b)
                    transposes(bank_b, y0[bp]).then_inc(pe_y0t, 1)
                if c is not None:
                    pe.wait_ge(ve_y1, c + 1)
                    if e is not None and old(e, 1):
                        pe.wait_ge(ac_gelu, 2 * e)
                    transposes(bank_c, y1).then_inc(pe_y1t, 1)
                if e is not None:
                    pe.wait_ge(ve_y3, e + 1)
                    if old(e, 1):
                        pe.wait_ge(ve_out, e)
                    transposes(bank_e, y3).then_inc(pe_y3t, 1)
                if x_ is not None:
                    experts(x_, xp, 0)
                if d is not None:
                    pe.wait_ge(ac_y2, d + 1)
                    if old(d, 1):
                        pe.wait_ge(ve_h3, d)
                    for t in range(2):
                        last = pe.matmul(bank_d2[:, 0:2], mean_w[:, :], clip_sums[:, t, :],
                                         start=(t == 0), stop=(t == 1))
                    last.then_inc(pe_clip, 1)
                    transposes(bank_d, y2).then_inc(pe_y2t, 1)
                if a is not None:
                    pe.wait_ge(ac_frame_t, a + 1)
                    pe.matmul(bank_a[0:2 * BINS, 0:TOKENS], dft_sb[:, :], frame_t[:, :],
                              start=True, stop=True).then_inc(pe_dft, 1)
                if c is not None:
                    pe.wait_ge(ac_y1t, c + 1)
                    for t in range(2):
                        for k in range(2):
                            last = pe.matmul(bank_c[0:T, t * EXPERTS:(t + 1) * EXPERTS],
                                             y1_t[cp][0:rows(k), k, t * T:(t + 1) * T],
                                             router_sb[0:rows(k), k, :], start=(k == 0), stop=(k == 1))
                    last.then_inc(pe_router, 1)
                if e is not None:
                    pe.wait_ge(ac_y3t, e + 1)
                    for t in range(2):
                        for k in range(2):
                            last = pe.matmul(bank_e[0:T, t * EXPERTS:(t + 1) * EXPERTS],
                                             y3_t[0:rows(k), k, t * T:(t + 1) * T],
                                             switch_sb[0:rows(k), k, :], start=(k == 0), stop=(k == 1))
                    last.then_inc(pe_switch, 1)
                if b is not None:
                    pe.wait_ge(ac_y0t, b + 1)
                    for t in range(2):
                        for k in range(2):
                            last = pe.matmul(bank_b[0:T, t * QUERIES:(t + 1) * QUERIES],
                                             y0_t[:, k, t * T:(t + 1) * T], y0_t[:, k, 0:QUERIES],
                                             start=(k == 0), stop=(k == 1))
                    last.then_inc(pe_scores_b, 1)
                if x_ is not None:
                    experts(x_, xp, 1)
                if a is not None:
                    pe.wait_ge(ac_power, a + 1)
                    pe.matmul(bank_a[0:MEL, 0:TOKENS], mel_sb[:, :], power[:, :],
                              start=True, stop=True).then_inc(pe_mel, 1)
                if d is not None:
                    pe.wait_ge(ve_xnt, d + 1)
                    for m in range(2):
                        for k in range(2):
                            last = pe.matmul(halves(bank_d, CH, TOKENS)[:, m, :],
                                             qk_sb[:, k, m * CH:(m + 1) * CH], xn_t[:, k, :],
                                             start=(k == 0), stop=(k == 1))
                    last.then_inc(pe_qk, 1)
                    for t in range(2):
                        for k in range(2):
                            last = pe.matmul(halves(bank_d2, T, C)[:, t, :], xn_t[:, k, t * T:(t + 1) * T],
                                             wv_sb[:, k, :], start=(k == 0), stop=(k == 1))
                    last.then_inc(pe_values, 1)
                if b is not None:
                    pe.wait_ge(ac_probs_b, b + 1)
                    for t in range(2):
                        last = pe.matmul(bank_b[0:QUERIES, 0:C + 1], probs_b[:, t, :], y0[bp][:, t, :],
                                         start=(t == 0), stop=(t == 1))
                    last.then_inc(pe_mix_b, 1)
                if x_ is not None:
                    experts(x_, xp, 2)
                if a is not None:
                    pe.wait_ge(ac_log, a + 1)
                    for t in range(2):
                        last = pe.matmul(halves(bank_a, T, C)[:, t, :], log_mel[:, t * T:(t + 1) * T],
                                         embed_sb[:, :], start=True, stop=True)
                    last.then_inc(pe_embed, 1)
                if e is not None:
                    pe.wait_ge(ve_hot, e + 1)
                    for t in range(2):
                        last = pe.transpose(bank_e[0:EXPERTS, t * T:(t + 1) * T], hot[:, t, :], ident_sb[0:T, 0:T])
                    last.then_inc(pe_hot_t, 1)
                if b is not None:
                    pe.wait_ge(ve_mix_b, b + 1)
                    for i in range(3):
                        kk = QUERIES + (i == 0)
                        last = pe.matmul(bank_b[0:QUERIES, 0:C], mix_b[0:kk, i:C:3],
                                         attn_sb[0:kk, i, :], start=(i == 0), stop=(i == 2))
                    last.then_inc(pe_proj_b, 1)
                if d is not None:
                    pe.wait_ge(ac_qk, d + 1)
                    for t in range(2):
                        for k in range(2):
                            last = pe.matmul(halves(bank_d, T, TOKENS)[:, t, :], qk_t[:, k, t * T:(t + 1) * T],
                                             xn_t[:, k, :], start=(k == 0), stop=(k == 1))
                    last.then_inc(pe_scores_d, 1)
                if x_ is not None:
                    experts(x_, xp, 3)
                for g in range(2):
                    if e is not None:
                        if g == 0:
                            pe.wait_ge(ve_hot_t, e + 1)
                            if c is not None:
                                pe.wait_ge(ve_mix_w, c + 1)
                        else:
                            pe.wait_ge(ve_masked, 2 * e + 1)
                        for m in range(2):
                            n = 2 * g + m
                            last = pe.matmul(halves(bank_e, 128, TOKENS)[:, m, :],
                                             rows_b[:, n * 128:(n + 1) * 128], hot_tb[:, :],
                                             start=True, stop=True)
                        last.then_inc(pe_mask, 1)
                        for m in range(2):
                            n = 2 * g + m
                            for k in range(2):
                                last = pe.matmul(halves(bank_c, 128, TOKENS)[:, m, :],
                                                 w1_sb[0:rows(k), k, n * 128:(n + 1) * 128],
                                                 y3_t[0:rows(k), k, :], start=(k == 0), stop=(k == 1))
                        last.then_inc(pe_hidden, 1)
                    if g == 0 and d is not None:
                        pe.wait_ge(ac_probs_d, 2 * d + 2)
                        for k in range(2):
                            for t in range(2):
                                last = pe.transpose(bank_d[0:T, k * TOKENS + t * T:k * TOKENS + (t + 1) * T],
                                                    probs_d[:, t, k * T:(k + 1) * T], ident_sb[0:T, 0:T])
                        last.then_inc(pe_probs_t, 1)
                    if x_ is not None:
                        experts(x_, xp, 4 + g)
                if d is not None:
                    pe.wait_ge(ve_probs_t, d + 1)
                    pe.wait_ge(ac_values, d + 1)
                    for t in range(2):
                        for k in range(2):
                            last = pe.matmul(halves(bank_d2, T, C)[:, t, :], probs_t[:, k, t * T:(t + 1) * T],
                                             values[:, k, :], start=(k == 0), stop=(k == 1))
                    last.then_inc(pe_mix_d, 1)
                if x_ is not None:
                    experts(x_, xp, 6)
                if e is not None:
                    pe.wait_ge(ve_masked, 2 * e + 2)
                    for t in range(2):
                        for n in range(4):
                            pe.matmul(halves(bank_e, T, C)[:, t, :], act_m[:, n, t * T:(t + 1) * T],
                                      w2_sb[:, n, :], start=(n == 0), stop=False)
                        last = pe.matmul(halves(bank_e, T, C)[:, t, :], hot_t[:, t * T:(t + 1) * T],
                                         b2_sb[:, :], start=False, stop=True)
                    last.then_inc(pe_out, 1)
                if x_ is not None:
                    experts(x_, xp, 7)

            run(pe, step)

        @block.vector
        def _(dve):
            dve.wait_ge(s_load, LOADED)
            dve.wait_ge(s_ones, 1)

            def statistics(k, src, b, own):
                for t in range(2):
                    dve.bn_stats(stats[k][:, t, :], src[:, t, :]).then_inc(ve_own, 1)
                dve.wait_ge(ve_own, own + 2)
                if old(b, 1):
                    dve.wait_ge(po_shift2 if k == 2 else po_rdev[k], b)
                settled(dve)
                for t in range(2):
                    last = dve.bn_aggr(moments[k][:, t, :], stats[k][:, t, :])
                last.then_inc(ve_moments[k], 1)

            def normalize(k, src, dst, b):
                dve.wait_ge(po_rdev[k], b + 1)
                for t in range(2):
                    last = dve.tensor_scalar(dst[:, t, 0:C], src[:, t, :], moments[k][:, t, 0:1],
                                             rdev[k][:, t:t + 1], ALU.subtract, ALU.mult)
                return last

            def combine(x_, xp, g):
                t, pair = g // 4, 2 * (g % 4)
                dve.wait_ge(pe_expert, 8 * x_ + g + 1)
                if g:
                    dve.wait_ge(ve_combined, 8 * x_ + g)
                dve.scalar_tensor_tensor(h2[xp][:, t, :], bank_x[g % 2][0:T, 0:C],
                                         mix_w[xp][:, t, pair:pair + 1], h2[xp][:, t, :],
                                         ALU.mult, ALU.add).then_inc(ve_pair, 1)
                dve.wait_ge(ve_pair, 8 * x_ + g + 1)
                dve.scalar_tensor_tensor(h2[xp][:, t, :], bank_x[g % 2][0:T, C:2 * C],
                                         mix_w[xp][:, t, pair + 1:pair + 2], h2[xp][:, t, :],
                                         ALU.mult, ALU.add).then_inc(ve_combined, 1)

            def step(j, par, clip):
                a, b, c, x_, d, e = (clip(s) for s in "ABCXDE")
                bp, xp, ep = ((par + STAGES[s]) % 2 for s in "BXE")
                dp = par
                own = own_before(j)
                if x_ is not None:
                    dve.wait_ge(po_h2, x_ + 1)
                    dve.wait_ge(ve_mix_w, x_ + 1)
                    combine(x_, xp, 0)
                if d is not None:
                    dve.wait_ge(pe_clip, d + 1)
                    dve.tensor_copy(clip_moments[:, :], bank_d2[:, 0:2]).then_inc(ve_own, 1)
                    dve.wait_ge(ve_own, own + 1)
                    dve.tensor_tensor(mean_sq[:, :], clip_moments[:, 0:1], clip_moments[:, 0:1],
                                      ALU.mult).then_inc(ve_own, 1)
                    dve.wait_ge(ve_own, own + 2)
                    dve.tensor_tensor(clip_var[:, :], clip_moments[:, 1:2], mean_sq[:, :],
                                      ALU.subtract).then_inc(ve_clip_var, 1)
                    own = own + 2
                if c is not None:
                    dve.wait_ge(pe_router, c + 1)
                    settled(dve)
                    for t in range(2):
                        dve.max(top[:, t, :], bank_c[0:T, t * EXPERTS:(t + 1) * EXPERTS]).then_inc(ve_own, 1)
                    dve.wait_ge(ve_own, own + 2)
                    dve.tensor_scalar(neg_top[:, :], top[:, :, 0], -1.0, None, ALU.mult).then_inc(ve_top, 1)
                    for t in range(2):
                        dve.max_index(top_at[:, t, :], top[:, t, :],
                                      bank_c[0:T, t * EXPERTS:(t + 1) * EXPERTS]).then_inc(ve_own, 1)
                    own = own + 4
                    dve.wait_ge(ve_own, own)
                    dve.tensor_tensor(pick_hot[:, :, :, :],
                                      iota_sb[0:T, :].unsqueeze(1).unsqueeze(1).to_broadcast([T, 2, 2, EXPERTS]),
                                      top_at[:, :, 0:2].unsqueeze(3).to_broadcast([T, 2, 2, EXPERTS]),
                                      ALU.is_equal).then_inc(ve_own, 1)
                    own = own + 1
                if e is not None:
                    dve.wait_ge(pe_switch, e + 1)
                    settled(dve)
                    for t in range(2):
                        dve.max(best[:, t, :], bank_e[0:T, t * EXPERTS:(t + 1) * EXPERTS]).then_inc(ve_own, 1)
                    dve.wait_ge(ve_own, own + 2)
                    dve.tensor_scalar(neg_best[:, :], best[:, :, 0], -1.0, None, ALU.mult).then_inc(ve_best, 1)
                    for t in range(2):
                        dve.max_index(best_at[:, t, :], best[:, t, :],
                                      bank_e[0:T, t * EXPERTS:(t + 1) * EXPERTS]).then_inc(ve_own, 1)
                    own = own + 4
                    dve.wait_ge(ve_own, own)
                    dve.tensor_tensor(hot[:, :, :],
                                      iota_sb[0:T, :].unsqueeze(1).to_broadcast([T, 2, EXPERTS]),
                                      best_at[:, :, 0:1].to_broadcast([T, 2, EXPERTS]),
                                      ALU.is_equal).then_inc(ve_hot, 1)
                if x_ is not None:
                    combine(x_, xp, 1)
                if d is not None:
                    dve.wait_ge(pe_y2t, d + 1)
                    dve.wait_ge(po_clip_rdev, d + 1)
                    dve.tensor_scalar(xn_t[:, :, :], halves(bank_d, CH, TOKENS), clip_moments[0:CH, 0:1],
                                      clip_rdev[0:CH, 0:1], ALU.subtract, ALU.mult).then_inc(ve_xnt, 1)
                if c is not None:
                    dve.wait_ge(ac_top_exp, 2 * c + 2)
                    dve.scalar_tensor_tensor(denom[:, :], exp_sum[:, :], 1e-9, top_exp[:, :, 1],
                                             ALU.mult, ALU.add).then_inc(ve_own, 1)
                    dve.wait_ge(ve_own, own + 1)
                    dve.tensor_tensor(denom1[:, :], denom[:, :], top_exp[:, :, 0], ALU.add).then_inc(ve_own, 1)
                    dve.wait_ge(ve_own, own + 2)
                    dve.reciprocal(rdenom[:, :], denom1[:, :]).then_inc(ve_own, 1)
                    dve.wait_ge(ve_own, own + 3)
                    dve.tensor_tensor(pick_w[:, :, :], top_exp[:, :, 0:2],
                                      rdenom[:, :].unsqueeze(2).to_broadcast([T, 2, 2]),
                                      ALU.mult).then_inc(ve_own, 1)
                    dve.wait_ge(ve_own, own + 4)
                    dve.tensor_tensor(pick_mix[:, :, :, :], pick_hot[:, :, :, :],
                                      pick_w[:, :, :].unsqueeze(3).to_broadcast([T, 2, 2, EXPERTS]),
                                      ALU.mult).then_inc(ve_own, 1)
                    dve.wait_ge(ve_own, own + 5)
                    own = own + 5
                    dve.tensor_tensor(mix_w[par][:, :, :], pick_mix[:, :, 0, :], pick_mix[:, :, 1, :],
                                      ALU.add).then_inc(ve_mix_w, 1)
                if b is not None:
                    dve.wait_ge(pe_mix_b, b + 1)
                    dve.reciprocal(rsum_b[:, :], bank_b[0:QUERIES, C:C + 1]).then_inc(ve_own, 1)
                    own = own + 1
                    dve.wait_ge(ve_own, own)
                    dve.tensor_scalar(mix_b[0:QUERIES, :], bank_b[0:QUERIES, 0:C], rsum_b[:, :], None,
                                      ALU.mult).then_inc(ve_mix_b, 1)
                if e is not None:
                    dve.wait_ge(pe_hot_t, e + 1)
                    dve.tensor_copy(hot_tb[:, :], bank_e[0:EXPERTS, 0:TOKENS])
                    dve.tensor_copy(hot_t[:, :], bank_e[0:EXPERTS, 0:TOKENS]).then_inc(ve_hot_t, 1)
                if x_ is not None:
                    combine(x_, xp, 2)
                if a is not None:
                    dve.wait_ge(pe_embed, a + 1)
                    if old(a, 2):
                        dve.wait_ge(po_h1, a - 1)
                    dve.tensor_copy(h0[par][:, :, :], halves(bank_a, T, C)).then_inc(ve_h0, 1)
                    dve.wait_ge(ve_h0, a + 1)
                    statistics(0, h0[par], a, own)
                    own = own + 2
                if x_ is not None:
                    combine(x_, xp, 3)
                if d is not None:
                    dve.wait_ge(pe_scores_d, d + 1)
                    for t in range(2):
                        last = dve.tensor_reduce(neg_max[:, t:t + 1], bank_d[0:T, t * TOKENS:(t + 1) * TOKENS],
                                                 AX_X, ALU.max, negate=True)
                    last.then_inc(ve_max_d, 1)
                if a is not None:
                    normalize(0, h0[par], y0[par], a).then_inc(ve_y0, 1)
                if b is not None:
                    dve.wait_ge(pe_proj_b, b + 1)
                    dve.wait_ge(po_h1, b + 1)
                    dve.tensor_tensor(h1[bp][0:QUERIES, 0, :], bank_b[0:QUERIES, 0:C], h0[bp][0:QUERIES, 0, :],
                                      ALU.add).then_inc(ve_h1, 1)
                    dve.wait_ge(ve_h1, b + 1)
                    statistics(1, h1[bp], b, own)
                    own = own + 2
                if x_ is not None:
                    combine(x_, xp, 4)
                if e is not None:
                    dve.wait_ge(pe_mask, 2 * e + 1)
                    dve.wait_ge(ac_gelu, 2 * e + 1)
                    dve.tensor_tensor(act_m[:, 0:2, :], act_h[:, 0:2, :], halves(bank_e, 128, TOKENS),
                                      ALU.mult).then_inc(ve_masked, 1)
                if d is not None:
                    dve.wait_ge(pe_probs_t, d + 1)
                    dve.tensor_copy(probs_t[:, :, :], halves(bank_d, T, TOKENS)).then_inc(ve_probs_t, 1)
                if b is not None:
                    if c is not None:
                        dve.wait_ge(pe_y1t, c + 1)
                    normalize(1, h1[bp], y1, b).then_inc(ve_y1, 1)
                if x_ is not None:
                    combine(x_, xp, 5)
                if e is not None:
                    dve.wait_ge(pe_mask, 2 * e + 2)
                    dve.wait_ge(ac_gelu, 2 * e + 2)
                    dve.tensor_tensor(act_m[:, 2:4, :], act_h[:, 2:4, :], halves(bank_e, 128, TOKENS),
                                      ALU.mult).then_inc(ve_masked, 1)
                if d is not None:
                    dve.wait_ge(pe_mix_d, d + 1)
                    dve.reciprocal(rsum_d[:, :], sum_d[:, :]).then_inc(ve_own, 1)
                    own = own + 1
                    dve.wait_ge(ve_own, own)
                    for t in range(2):
                        last = dve.scalar_tensor_tensor(h3[dp][:, t, :], halves(bank_d2, T, C)[:, t, :],
                                                        rsum_d[:, t:t + 1], h2[dp][:, t, :],
                                                        ALU.mult, ALU.add)
                    last.then_inc(ve_h3, 1)
                    dve.wait_ge(ve_h3, d + 1)
                    statistics(3, h3[dp], d, own)
                    own = own + 2
                if x_ is not None:
                    combine(x_, xp, 6)
                if d is not None:
                    if e is not None:
                        dve.wait_ge(pe_y3t, e + 1)
                    normalize(3, h3[dp], y3, d).then_inc(ve_y3, 1)
                if e is not None:
                    dve.wait_ge(ac_route_exp, 2 * e + 2)
                    dve.reciprocal(route_prob[:, :], route_sum[:, :]).then_inc(ve_own, 1)
                    own = own + 1
                    dve.wait_ge(ve_own, own)
                    dve.wait_ge(pe_out, e + 1)
                    if old(e, 2):
                        stored = (e // 2) * 16 if isinstance(e, int) else (e - (1 - par)) * 8
                        dve.wait_ge(s_stored[ep], stored)
                    for t in range(2):
                        last = dve.scalar_tensor_tensor(out_sb[ep][:, t, :], halves(bank_e, T, C)[:, t, :],
                                                        route_prob[:, t:t + 1], h3[ep][:, t, :],
                                                        ALU.mult, ALU.add)
                    last.then_inc(ve_out, 1)
                if x_ is not None:
                    combine(x_, xp, 7)
                    dve.wait_ge(ve_combined, 8 * x_ + 8)
                    statistics(2, h2[xp], x_, own)
                    own = own + 2

            OWN = {"A": 2, "B": 1 + 2, "C": 4 + 1 + 5, "X": 2, "D": 2 + 1 + 2, "E": 4 + 1}

            def own_before(j):
                if isinstance(j, int):
                    return sum(n * min(max(j - STAGES[s], 0), CLIPS) for s, n in OWN.items())
                return j * sum(OWN.values()) - sum(n * STAGES[s] for s, n in OWN.items())

            run(dve, step)


def kernel(**inputs):
    import numpy as np
    import concourse.bacc as bacc
    from concourse.bass_utils import run_bass_kernel_spmd

    def rows(*parts):
        return np.concatenate([np.atleast_2d(p) for p in parts], axis=0)

    given = {k: np.asarray(v) for k, v in inputs.items()}
    n = np.arange(FRAME)
    window = (0.54 - 0.46 * np.cos(2.0 * np.pi * n / (FRAME - 1))).astype(np.float32).astype(np.float64)
    angle = 2.0 * np.pi * ((n[:, None] * np.arange(BINS)[None, :]) % FRAME) / FRAME
    dft = np.concatenate([window[:, None] * np.cos(angle), -window[:, None] * np.sin(angle)], axis=1)
    one_hot_row = np.zeros((1, MEL + 1), np.float32)
    one_hot_row[0, MEL] = 1.0
    enc_row = np.zeros((1, C + 1), np.float32)
    enc_row[0, C] = 1.0
    g = given
    arrays = {
        "x": g["x"],
        "dft": dft.astype(np.float32),
        "ident": np.eye(128, dtype=np.float32),
        "iota": np.tile(np.arange(EXPERTS, dtype=np.float32), (128, 1)),
        "expert_rows": np.repeat(np.eye(EXPERTS, dtype=np.float32), HID, axis=1),
        "mel_w": rows(g["L0_tok_mel_filters"].T, g["L0_tok_mel_filters"].T),
        "dct_w": rows(np.concatenate([g["L0_tok_dct"], np.zeros((MFCC, 1), np.float32)], axis=1), one_hot_row),
        "embed_w": rows(g["L0_tok_w_proj"], g["L0_tok_b_proj"]),
        "attn_w": g["L0_attn_proj_w"].T,
        "attn_b": g["L0_attn_proj_b"][None, :],
        "router_w": rows(g["L0_ffn_router_w"].T, g["L0_ffn_router_b"]),
        "expert_w": rows(g["L0_ffn_expert_w"].transpose(2, 0, 1).reshape(C, EXPERTS * C),
                         g["L0_ffn_expert_b"].reshape(1, EXPERTS * C)),
        "wq": g["L1_attn_Wq"],
        "wk": g["L1_attn_Wk"],
        "wv": g["L1_attn_Wv"].T,
        "enc_w": rows(np.concatenate([g["L1_ffn_enc_w"].T, g["L1_ffn_enc_b"][:, None]], axis=1), enc_row),
        "switch_w": rows(g["L1_ffn_sw_w"], g["L1_ffn_sw_b"]),
        "w1": rows(g["L1_ffn_w1"].transpose(1, 0, 2).reshape(C, EXPERTS * HID),
                   g["L1_ffn_b1"].reshape(1, EXPERTS * HID)),
        "w2": g["L1_ffn_w2"].reshape(EXPERTS * HID, C),
        "b2": g["L1_ffn_b2"],
    }
    arrays = {f"in_{k}": np.ascontiguousarray(v) for k, v in arrays.items()}
    nc = bacc.Bacc("TRN2", target_bir_lowering=False, num_devices=1)
    args = [nc.dram_tensor(k, v.shape, mybir.dt.from_np(v.dtype), kind="ExternalInput").ap()
            for k, v in arrays.items()]
    out = nc.dram_tensor("out_0", (CLIPS, TOKENS, C), F32, kind="ExternalOutput").ap()
    tower(nc, *args, out)
    result = run_bass_kernel_spmd(nc, [arrays], core_ids=[0])
    return result.results[0]["out_0"]
```

```python
from contextlib import ExitStack

import concourse.bass as bass
from concourse import mybir

ALU = mybir.AluOpType
ACT = mybir.ActivationFunctionType
F32 = mybir.dt.float32
F16 = mybir.dt.float16
U32 = mybir.dt.uint32
AX_X = mybir.AxisListType.X

CLIPS, AUDIO = 32, 40000
FRAME, HOP = 100, 160
TOKENS = 1 + (AUDIO - FRAME) // HOP
T = TOKENS // 2
BINS = FRAME // 2 + 1
MEL, MFCC = 40, 13
C = 192
CH = C // 2
QUERIES = 64
EXPERTS = 8
HID = 64
EPS = 1e-5
KA = 128
KB = C - KA
BIAS_H, BIAS_L = 64, 96
KG = BIAS_L + 1
EXPERT_SCALE = 64.0
HIDDEN_SCALE = 16.0
VALUE_SCALE = 64.0
PAIR = 2 * C

STAGES = {"A": 0, "L": 1, "B": 2, "C": 3, "X": 4, "N": 5, "D": 6, "E": 7, "S": 8}
LAST = STAGES["S"]
FIRST_LOOPED = 10
END_LOOPED = CLIPS


def tower(nc, x, dft, ident, iota, expert_rows, mel_w, dct_w, embed_w, attn_w, attn_b,
          router_w, expert_w, wq, wk, wv, enc_w, switch_w, w1, w2, b2, out):
    frames = x.rearrange("b (t p n) -> b p t n", t=2, n=HOP)
    out_tokens = out.rearrange("b (t p) c -> b p t c", t=2)

    with ExitStack() as ctx:
        def sb(name, shape, dt=F32):
            return ctx.enter_context(nc.sbuf_tensor(name, shape, dt))

        def ps(name, shape, dt=F32):
            return ctx.enter_context(nc.psum_tensor(name, shape, dt))

        def sem(name):
            return ctx.enter_context(nc.semaphore(name))

        dft_sb = sb("dft_sb", [FRAME, 2 * BINS])
        ident_sb = sb("ident_sb", [128, 128])
        iota_sb = sb("iota_sb", [128, EXPERTS])
        rows_f = sb("rows_f", [EXPERTS, EXPERTS * HID])
        rows_h = sb("rows_h", [EXPERTS, EXPERTS * HID], F16)
        mel_sb = sb("mel_sb", [2 * BINS, MEL])
        dct_sb = sb("dct_sb", [MFCC + 1, MEL + 1])
        embed_in = sb("embed_in", [MFCC + 1, C])
        embed_sb = sb("embed_sb", [MEL + 1, C])
        attn_sb = sb("attn_sb", [QUERIES + 1, 3, C])
        router_f = sb("router_f", [128, 3, EXPERTS])
        router_h = sb("router_h", [128, 4, EXPERTS], F16)
        expert_f = sb("expert_f", [128, 3, EXPERTS * C])
        expert_h = sb("expert_h", [128, 4, EXPERTS * C], F16)
        w1_f = sb("w1_f", [128, 3, EXPERTS * HID])
        w1_h = sb("w1_h", [128, 4, EXPERTS * HID], F16)
        wv_f = sb("wv_f", [128, 2, C])
        wv_h = sb("wv_h", [128, 4, C], F16)
        qk_f = sb("qk_f", [128, 2, 256])
        qk_h = sb("qk_h", [128, 4, 256], F16)
        switch_f = sb("switch_f", [128, 3, EXPERTS])
        switch_h = sb("switch_h", [128, 4, EXPERTS], F16)
        wq_sb = sb("wq_sb", [CH, 2, C])
        wk_sb = sb("wk_sb", [CH, 2, C])
        enc_sb = sb("enc_sb", [HID + 1, C + 1])
        switch_in = sb("switch_in", [HID + 1, EXPERTS])
        w2_sb = sb("w2_sb", [128, 4, C])
        b2_f = sb("b2_f", [72, C])
        b2_part = [sb(f"b2_part{i}", [72, C], F16) for i in range(3)]
        b2_rest = [sb(f"b2_rest{i}", [72, C]) for i in range(2)]
        b2_h = sb("b2_h", [72, C], F16)
        mean_w = sb("mean_w", [T, 128])
        log_eps = sb("log_eps", [128, 1])
        minus_half = sb("minus_half", [128, 2])

        frame_sb = [sb(f"frame_sb{i}", [T, 2, FRAME]) for i in range(2)]
        frame_t = sb("frame_t", [FRAME, TOKENS])
        power = sb("power", [2 * BINS, TOKENS])
        log_mel = sb("log_mel", [MEL + 1, TOKENS])
        h0 = [sb(f"h0_{i}", [T, 2, C]) for i in range(2)]
        stats = [sb(f"stats{k}", [T, 2, 6]) for k in range(4)]
        moments = [sb(f"moments{k}", [T, 2, 2]) for k in range(4)]
        var_eps = [sb(f"var_eps{k}", [T, 2]) for k in range(4)]
        rdev = [sb(f"rdev{k}", [T, 2]) for k in range(4)]
        y0 = [sb(f"y0_{i}", [T, 2, C + 1]) for i in range(2)]
        y0_t = sb("y0_t", [CH, 2, TOKENS])
        probs_b = sb("probs_b", [T, 2, QUERIES])
        rsum_b = sb("rsum_b", [QUERIES, 1])
        mix_b = sb("mix_b", [QUERIES + 1, C])
        h1 = [sb(f"h1_{i}", [T, 2, C]) for i in range(2)]
        y1 = sb("y1", [T, 2, C])
        y1_s = [sb(f"y1_s{i}", [128, 3, TOKENS], F16) for i in range(2)]
        y1_g = [sb(f"y1_g{i}", [128, TOKENS], F16) for i in range(2)]
        top = sb("top", [T, 2, 8])
        top_at = sb("top_at", [T, 2, 8], U32)
        neg_top = sb("neg_top", [T, 2])
        top_exp = sb("top_exp", [T, 2, 8])
        exp_sum = sb("exp_sum", [T, 2])
        denom = sb("denom", [T, 2])
        denom1 = sb("denom1", [T, 2])
        rdenom = sb("rdenom", [T, 2])
        pick_w = sb("pick_w", [T, 2, 2])
        pick_hot = sb("pick_hot", [T, 2, 2, EXPERTS])
        pick_mix = sb("pick_mix", [T, 2, 2, EXPERTS])
        mix_w = [sb(f"mix_w{i}", [T, 2, EXPERTS]) for i in range(2)]
        h2 = [sb(f"h2_{i}", [T, 2, C]) for i in range(2)]
        shift2 = sb("shift2", [T, 2])
        y2 = sb("y2", [T, 2, C])
        y2_sq = sb("y2_sq", [T, 2, C])
        clip_sums = sb("clip_sums", [T, 2, 2])
        clip_moments = sb("clip_moments", [128, 2])
        mean_sq = sb("mean_sq", [128, 1])
        clip_var = sb("clip_var", [128, 1])
        clip_var_eps = sb("clip_var_eps", [128, 1])
        clip_rdev = sb("clip_rdev", [128, 1])
        clip_mean = sb("clip_mean", [128, 1])
        clip_shift = sb("clip_shift", [128, 1])
        xn = sb("xn", [T, 2, C])
        xn_s = sb("xn_s", [128, 3, TOKENS], F16)
        qk_th = sb("qk_th", [128, 2, TOKENS], F16)
        qk_tl = sb("qk_tl", [128, 2, TOKENS], F16)
        values = sb("values", [T, 2, C])
        neg_max = sb("neg_max", [T, 2])
        probs_d = sb("probs_d", [T, 2, TOKENS])
        probs_t = sb("probs_t", [T, 2, TOKENS])
        sum_d = sb("sum_d", [T, 2])
        rsum_d = sb("rsum_d", [T, 2])
        h3 = [sb(f"h3_{i}", [T, 2, C]) for i in range(2)]
        y3 = sb("y3", [T, 2, C])
        y3_s = sb("y3_s", [128, 3, TOKENS], F16)
        y3_g = sb("y3_g", [128, TOKENS], F16)
        best = sb("best", [T, 2, 8])
        best_at = sb("best_at", [T, 2, 8], U32)
        neg_best = sb("neg_best", [T, 2])
        route_exp = sb("route_exp", [T, 2, 8])
        route_sum = sb("route_sum", [T, 2])
        route_prob = sb("route_prob", [T, 2])
        hot = sb("hot", [T, 2, 96])
        hot_t = sb("hot_t", [72, TOKENS], F16)
        act_h = sb("act_h", [128, 4, TOKENS])
        act_m = sb("act_m", [128, 4, TOKENS])
        out_sb = [sb(f"out_sb{i}", [T, 2, C]) for i in range(2)]

        bank_a = ps("bank_a", [128, 512])
        bank_b = ps("bank_b", [128, 512])
        bank_c = ps("bank_c", [128, 512])
        bank_d = ps("bank_d", [128, 512])
        bank_d2 = ps("bank_d2", [128, 512])
        bank_e = ps("bank_e", [128, 512])
        bank_x = [ps(f"bank_x{i}", [128, 512]) for i in range(2)]

        def halves(bank, rows, n):
            return bank[0:rows, 0:2 * n].rearrange("p (t n) -> p t n", t=2)

        s_load = sem("s_load")
        s_ones = sem("s_ones")
        s_high = sem("s_high")
        s_split = sem("s_split")
        s_b2 = sem("s_b2")
        s_zero = sem("s_zero")
        s_fold = sem("s_fold")
        s_folded = sem("s_folded")
        s_frames = [sem(f"s_frames{i}") for i in range(2)]
        s_stored = [sem(f"s_stored{i}") for i in range(2)]
        pe_frames, pe_dft, pe_mel, pe_embed = (sem(n) for n in ("pe_frames", "pe_dft", "pe_mel", "pe_embed"))
        pe_y0t, pe_scores_b, pe_mix_b, pe_proj_b = (sem(n) for n in ("pe_y0t", "pe_scores_b", "pe_mix_b", "pe_proj_b"))
        pe_y1t, pe_router, pe_expert = (sem(n) for n in ("pe_y1t", "pe_router", "pe_expert"))
        pe_clip, pe_y2t, pe_qk, pe_values, pe_scores_d, pe_probs_t, pe_mix_d = (
            sem(n) for n in ("pe_clip", "pe_y2t", "pe_qk", "pe_values", "pe_scores_d", "pe_probs_t", "pe_mix_d"))
        pe_y3t, pe_switch, pe_hot_t, pe_mask, pe_hidden, pe_out = (
            sem(n) for n in ("pe_y3t", "pe_switch", "pe_hot_t", "pe_mask", "pe_hidden", "pe_out"))
        ac_frame_t, ac_power, ac_log, ac_y0t, ac_probs_b, ac_y1g, ac_top_exp = (
            sem(n) for n in ("ac_frame_t", "ac_power", "ac_log", "ac_y0t", "ac_probs_b", "ac_y1g", "ac_top_exp"))
        ac_y2, ac_xn, ac_xnt, ac_qk, ac_values, ac_probs_d, ac_y3g, ac_route_exp, ac_gelu = (
            sem(n) for n in ("ac_y2", "ac_xn", "ac_xnt", "ac_qk", "ac_values", "ac_probs_d", "ac_y3g", "ac_route_exp", "ac_gelu"))
        ve_h0, ve_y0, ve_mix_b, ve_h1, ve_y1, ve_top, ve_mix_w, ve_pair, ve_combined = (
            sem(n) for n in ("ve_h0", "ve_y0", "ve_mix_b", "ve_h1", "ve_y1", "ve_top", "ve_mix_w", "ve_pair", "ve_combined"))
        ve_y1s, ve_y3s, ve_qk = (sem(n) for n in ("ve_y1s", "ve_y3s", "ve_qk"))
        ve_clip_var, ve_xnt, ve_max_d, ve_probs_t, ve_h3, ve_y3, ve_best, ve_hot, ve_hot_t, ve_masked, ve_out = (
            sem(n) for n in ("ve_clip_var", "ve_xnt", "ve_max_d", "ve_probs_t", "ve_h3", "ve_y3", "ve_best", "ve_hot",
                             "ve_hot_t", "ve_masked", "ve_out"))
        ve_moments = [sem(f"ve_moments{k}") for k in range(4)]
        ve_own = sem("ve_own")
        po_rdev = [sem(f"po_rdev{k}") for k in range(4)]
        po_shift2, po_h1, po_h3, po_clip_rdev, po_own = (
            sem(n) for n in ("po_shift2", "po_h1", "po_h3", "po_clip_rdev", "po_own"))

        block = ctx.enter_context(nc.Block())

        def run(eng, step):
            def at(j):
                def clip(stage):
                    b = j - STAGES[stage]
                    return b if 0 <= b < CLIPS else None
                step(j, j % 2, clip)

            for j in range(FIRST_LOOPED):
                at(j)
            with eng.Fori(FIRST_LOOPED, END_LOOPED - 1, 2) as i:
                for par in range(2):
                    step(i + par, par, lambda stage, par=par: i + (par - STAGES[stage]))
            for j in range(END_LOOPED, CLIPS + LAST):
                at(j)

        def settled(eng):
            eng.nop(nofuse=True)

        def before(counts, j):
            if isinstance(j, int):
                return sum(n * min(max(j - STAGES[s], 0), CLIPS) for s, n in counts.items())
            return j * sum(counts.values()) - sum(n * STAGES[s] for s, n in counts.items())

        def old(b, back):
            return not isinstance(b, int) or b >= back

        LOADS_SP = [
            (ident_sb[:, :], ident), (dft_sb[:, :], dft), (mel_sb[:, :], mel_w), (dct_sb[:, :], dct_w),
            (embed_in[:, :], embed_w), (iota_sb[:, :], iota), (rows_f[:, :], expert_rows),
            (attn_sb[0:QUERIES, :, :], attn_w.rearrange("(a q) o -> q a o", q=QUERIES)),
            (attn_sb[QUERIES:QUERIES + 1, 0, :], attn_b),
            (enc_sb[:, :], enc_w), (switch_in[:, :], switch_w),
            (wq_sb[:, :, :], wq.rearrange("(t p) n -> p t n", t=2)),
            (wk_sb[:, :, :], wk.rearrange("(t p) n -> p t n", t=2)),
            (w2_sb[:, :, :], w2.rearrange("(t p) n -> p t n", t=4)),
        ]
        for dst, src in ((router_f, router_w), (wv_f, wv), (w1_f, w1), (expert_f, expert_w)):
            LOADS_SP += [(dst[:, 0, :], src[0:KA, :]), (dst[0:KB, 1, :], src[KA:C, :]),
                         (dst[KB:128, 1, :], src[KA:C, :])]
            if src.shape[0] > C:
                LOADS_SP += [(dst[p:p + 1, 2, :], src[C:C + 1, :]) for p in (BIAS_H, BIAS_L)]
        B2_LOADS = [(b2_f[p:p + EXPERTS, :], b2) for p in (0, 32, 64)]
        LOADED = 16 * len(LOADS_SP)
        SPLITS = [(router_f, router_h, EXPERT_SCALE, True), (wv_f, wv_h, VALUE_SCALE, False),
                  (w1_f, w1_h, HIDDEN_SCALE, True), (expert_f, expert_h, EXPERT_SCALE, True),
                  (qk_f, qk_h, 1.0, False), (switch_f, switch_h, 1.0, True)]

        @block.sync
        def _(sp):
            for dst, src in LOADS_SP:
                sp.dma_start(dst, src).then_inc(s_load, 16)
            sp.wait_ge(s_zero, 1)
            for dst, src in B2_LOADS:
                sp.dma_start(dst, src).then_inc(s_b2, 16)

            def step(j, par, clip):
                a, e = clip("A"), clip("S")
                if a is not None:
                    if old(a, 2):
                        sp.wait_ge(pe_frames, a - 1)
                    src = frames[a] if isinstance(a, int) else frames[bass.ds(a, 1)].rearrange(
                        "a p t n -> (a p) t n")
                    sp.dma_start(frame_sb[par][:, :, :], src[:, :, 0:FRAME]).then_inc(s_frames[par], 16)
                if e is not None:
                    sp.wait_ge(ve_out, e + 1)
                    dst = out_tokens[e] if isinstance(e, int) else out_tokens[bass.ds(e, 1)].rearrange(
                        "a p t c -> (a p) t c")
                    ep = (par + STAGES["S"]) % 2
                    sp.dma_start(dst, out_sb[ep][:, :, :]).then_inc(s_stored[ep], 16)

            run(sp, step)
            for i in range(2):
                sp.wait_ge(s_stored[i], 16 * (CLIPS // 2))


        @block.gpsimd
        def _(pool):
            pool.memset(log_eps[:, :], 1e-6)
            pool.memset(minus_half[:, :], -0.5)
            pool.memset(mean_w[:, :], 1.0 / (TOKENS * C))
            pool.memset(log_mel[:, :], 1.0)
            pool.memset(mix_b[:, :], 1.0)
            pool.memset(probs_b[:, :, :], 0.0)
            pool.memset(b2_f[:, :], 0.0).then_inc(s_zero, 1)
            pool.memset(b2_h[:, :], 0.0)
            pool.memset(hot[:, :, :], 0.0)
            for parts in (router_h, expert_h, w1_h, switch_h):
                pool.memset(parts[:, 3, :], 0.0)
            for i in range(2):
                pool.memset(y0[i][:, :, :], 1.0)
            for g in (y1_g[0], y1_g[1], y3_g):
                pool.memset(g[:, :], 0.0)
            pool.memset(neg_top[:, :], 0.0).then_inc(s_ones, 1)
            pool.wait_ge(s_ones, 1)

            def layernorm(k, b):
                pool.wait_ge(ve_moments[k], b + 1)
                settled(pool)
                pool.tensor_scalar(var_eps[k][:, :], moments[k][:, :, 1], EPS, None,
                                   ALU.add).then_inc(po_own, 1)

            def power_minus_half(k):
                pool.tensor_tensor(rdev[k][:, :], var_eps[k][:, :], minus_half[0:T, :],
                                   ALU.pow).then_inc(po_rdev[k], 1)

            def step(j, par, clip):
                l, b, x_, n, d = (clip(s) for s in "LBXND")
                bp, dp = ((par + STAGES[s]) % 2 for s in "BD")
                own = pool_own_before(j)
                if d is not None:
                    pool.wait_ge(ve_combined, 8 * d + 8)
                    if old(d, 2):
                        pool.wait_ge(ve_out, d - 1)
                    settled(pool)
                    pool.tensor_copy(h3[dp][:, :, :], h2[dp][:, :, :]).then_inc(po_h3, 1)
                if n is not None:
                    pool.wait_ge(ve_clip_var, n + 1)
                    if old(n, 1):
                        pool.wait_ge(ac_xn, n)
                    settled(pool)
                    pool.tensor_scalar(clip_var_eps[:, :], clip_var[:, :], EPS, None,
                                       ALU.add).then_inc(po_own, 1)
                    pool.wait_ge(po_own, own + 1)
                    pool.tensor_tensor(clip_rdev[:, :], clip_var_eps[:, :], minus_half[:, 0:1],
                                       ALU.pow).then_inc(po_own, 1)
                    pool.wait_ge(po_own, own + 2)
                    pool.tensor_tensor(clip_mean[:, :], clip_moments[:, 0:1], clip_rdev[:, :],
                                       ALU.mult).then_inc(po_own, 1)
                    own = own + 3
                    pool.wait_ge(po_own, own)
                    settled(pool)
                    pool.tensor_scalar(clip_shift[:, :], clip_mean[:, :], -1.0, None,
                                       ALU.mult).then_inc(po_clip_rdev, 1)
                if l is not None:
                    layernorm(0, l)
                    own = own + 1
                    pool.wait_ge(po_own, own)
                    power_minus_half(0)
                if b is not None:
                    pool.wait_ge(ve_y0, b + 1)
                    if old(b, 2):
                        pool.wait_ge(ve_pair, 8 * b - 11)
                        pool.wait_ge(ve_y1, b - 1)
                    pool.tensor_tensor(h1[bp][:, :, :], h0[bp][:, :, :], y0[bp][:, :, 0:C],
                                       ALU.add).then_inc(po_h1, 1)
                    layernorm(1, b)
                    own = own + 1
                    pool.wait_ge(po_own, own)
                    power_minus_half(1)
                if d is not None:
                    layernorm(3, d)
                    own = own + 1
                    pool.wait_ge(po_own, own)
                    power_minus_half(3)
                if x_ is not None:
                    if old(x_, 1):
                        pool.wait_ge(ac_y2, x_)
                    layernorm(2, x_)
                    own = own + 1
                    pool.wait_ge(po_own, own)
                    power_minus_half(2)
                    pool.wait_ge(po_rdev[2], x_ + 1)
                    pool.tensor_tensor(shift2[:, :], moments[2][:, :, 0], rdev[2][:, :],
                                       ALU.mult).then_inc(po_own, 1)
                    own = own + 1
                    pool.wait_ge(po_own, own)
                    settled(pool)
                    pool.tensor_scalar(shift2[:, :], shift2[:, :], -1.0, None,
                                       ALU.mult).then_inc(po_shift2, 1)

            OWN = {"L": 1, "B": 1, "N": 3, "D": 1, "X": 2}

            def pool_own_before(j):
                return before(OWN, j)

            run(pool, step)

        @block.scalar
        def _(act):
            act.wait_ge(s_load, LOADED)
            act.wait_ge(s_ones, 1)
            act.activation(rows_h[:, :], rows_f[:, :], ACT.Copy).then_inc(s_folded, 1)
            act.wait_ge(s_fold, 1)
            act.activation(embed_sb[:, :], bank_a[0:MEL + 1, 0:C], ACT.Copy).then_inc(s_folded, 1)
            for n, bank in ((0, bank_b), (1, bank_d)):
                act.activation(qk_f[:, n, 0:C], bank[:, 0:C], ACT.Copy)
                act.activation(qk_f[:, n, C:256], bank[:, KA:C], ACT.Copy).then_inc(s_folded, 1)
            act.activation(switch_f[:, 0, :], bank_c[:, 0:EXPERTS], ACT.Copy)
            act.activation(switch_f[:, 1, :], bank_c[:, EXPERTS:2 * EXPERTS], ACT.Copy)
            for p in (BIAS_H, BIAS_L):
                last = act.activation(switch_f[p:p + 1, 2, :], bank_e[p:p + 1, 0:EXPERTS], ACT.Copy)
            last.then_inc(s_folded, 1)
            act.wait_ge(s_folded, 5)
            for full, parts, scale, bias in SPLITS:
                act.activation(parts[:, 0, :], full[:, 0, :], ACT.Copy, scale=scale)
                last = act.activation(parts[:, 2, :], full[:, 1, :], ACT.Copy, scale=scale)
                if bias:
                    for p in (BIAS_H, BIAS_L):
                        last = act.activation(parts[p:p + 1, 3, :], full[p:p + 1, 2, :], ACT.Copy, scale=scale)
                last.then_inc(s_high, 1)

            def step(j, par, clip):
                a, l, b, c, x_, n, d, e = (clip(s) for s in "ALBCXNDE")
                cp, np_ = ((par + STAGES[s]) % 2 for s in "CN")
                if l is not None:
                    act.wait_ge(pe_mel, l + 1)
                    act.activation(log_mel[0:MEL, :], bank_a[0:MEL, 0:TOKENS], ACT.Ln,
                                   bias=log_eps[0:MEL, :]).then_inc(ac_log, 1)
                if b is not None:
                    act.wait_ge(pe_y0t, b + 1)
                    act.activation(y0_t[:, :, :], halves(bank_b, CH, TOKENS), ACT.Copy).then_inc(ac_y0t, 1)
                if c is not None:
                    act.wait_ge(pe_y1t, c + 1)
                    if old(c, 2):
                        act.wait_ge(pe_expert, 8 * (c - 1))
                    act.activation(y1_s[cp][:, 0:2, :], halves(bank_c, 128, TOKENS), ACT.Copy)
                    act.activation(y1_g[cp][0:KB, :], bank_c[KB:128, TOKENS:2 * TOKENS],
                                   ACT.Copy).then_inc(ac_y1g, 1)
                if d is not None:
                    act.wait_ge(pe_y2t, d + 1)
                    act.activation(xn_s[:, 0:2, :], halves(bank_d, 128, TOKENS), ACT.Copy).then_inc(ac_xnt, 1)
                if e is not None:
                    act.wait_ge(pe_y3t, e + 1)
                    act.activation(y3_s[:, 0:2, :], halves(bank_e, 128, TOKENS), ACT.Copy)
                    act.activation(y3_g[0:KB, :], bank_e[KB:128, TOKENS:2 * TOKENS], ACT.Copy).then_inc(ac_y3g, 1)
                if n is not None:
                    act.wait_ge(ve_combined, 8 * n + 8)
                    act.wait_ge(po_shift2, n + 1)
                    if old(n, 1):
                        act.wait_ge(pe_clip, n)
                    for t in range(2):
                        act.activation(y2[:, t, :], h2[np_][:, t, :], ACT.Identity, scale=rdev[2][:, t:t + 1],
                                       bias=shift2[:, t:t + 1], accum_out=clip_sums[:, t, 0:1])
                        last = act.activation(y2_sq[:, t, :], h2[np_][:, t, :], ACT.Square,
                                              scale=rdev[2][:, t:t + 1], bias=shift2[:, t:t + 1],
                                              accum_out=clip_sums[:, t, 1:2])
                    last.then_inc(ac_y2, 1)
                if a is not None:
                    act.wait_ge(pe_frames, a + 1)
                    act.activation(frame_t[:, :], bank_a[0:FRAME, 0:TOKENS], ACT.Copy).then_inc(ac_frame_t, 1)
                if c is not None:
                    act.wait_ge(ve_top, c + 1)
                    for t in range(2):
                        act.activation(top_exp[:, t, :], top[:, t, :], ACT.Exp, bias=neg_top[:, t:t + 1],
                                       scale=1.0 / EXPERT_SCALE, accum_out=exp_sum[:, t:t + 1]).then_inc(ac_top_exp, 1)
                if e is not None:
                    act.wait_ge(ve_best, e + 1)
                    for t in range(2):
                        act.activation(route_exp[:, t, :], best[:, t, :], ACT.Exp, bias=neg_best[:, t:t + 1],
                                       accum_out=route_sum[:, t:t + 1]).then_inc(ac_route_exp, 1)
                if b is not None:
                    act.wait_ge(pe_scores_b, b + 1)
                    act.activation(probs_b[QUERIES:T, 0, :], bank_b[QUERIES:T, 0:QUERIES], ACT.Exp,
                                   scale=0.25)
                    act.activation(probs_b[:, 1, :], bank_b[0:T, QUERIES:2 * QUERIES], ACT.Exp,
                                   scale=0.25).then_inc(ac_probs_b, 1)
                if n is not None:
                    act.wait_ge(po_clip_rdev, n + 1)
                    if old(n, 1):
                        act.wait_ge(pe_y2t, n)
                    for t in range(2):
                        last = act.activation(xn[:, t, :], y2[:, t, :], ACT.Identity, scale=clip_rdev[0:T, :],
                                              bias=clip_shift[0:T, :])
                    last.then_inc(ac_xn, 1)
                if a is not None:
                    act.wait_ge(pe_dft, a + 1)
                    act.activation(power[:, :], bank_a[0:2 * BINS, 0:TOKENS], ACT.Square).then_inc(ac_power, 1)
                if d is not None:
                    act.wait_ge(pe_qk, d + 1)
                    act.activation(qk_th[:, :, :], halves(bank_d, 128, TOKENS), ACT.Copy).then_inc(ac_qk, 1)
                    act.wait_ge(pe_values, d + 1)
                    act.activation(values[:, :, :], halves(bank_d2, T, C), ACT.Copy,
                                   scale=1.0 / VALUE_SCALE).then_inc(ac_values, 1)
                    act.wait_ge(ve_max_d, d + 1)
                    if old(d, 1):
                        act.wait_ge(ve_h3, d)
                    for t in range(2):
                        act.activation(probs_d[:, t, :], bank_d[0:T, t * TOKENS:(t + 1) * TOKENS], ACT.Exp,
                                       bias=neg_max[:, t:t + 1],
                                       accum_out=sum_d[:, t:t + 1]).then_inc(ac_probs_d, 1)
                if e is not None:
                    for g in range(2):
                        act.wait_ge(pe_hidden, 2 * e + g + 1)
                        act.activation(act_h[:, 2 * g:2 * g + 2, :], halves(bank_c, 128, TOKENS),
                                       ACT.Gelu, scale=1.0 / HIDDEN_SCALE).then_inc(ac_gelu, 1)

            run(act, step)

        @block.tensor
        def _(pe):
            pe.wait_ge(s_load, LOADED)
            pe.wait_ge(s_ones, 1)
            pe.matmul(bank_a[0:MEL + 1, 0:C], dct_sb[:, :], embed_in[:, :], start=True, stop=True)
            for bank, m0, m1 in ((bank_b, 0, KA), (bank_d, KA, C)):
                for p in range(0, 128, m1 - m0):
                    for k in range(2):
                        pe.matmul(bank[p:p + m1 - m0, 0:C], wq_sb[:, k, m0:m1], wk_sb[:, k, :],
                                  start=(k == 0), stop=(k == 1))
            pe.matmul(bank_c[:, 0:EXPERTS], enc_sb[:, 0:KA], switch_in[:, :], start=True, stop=True)
            for p in (0, KB):
                pe.matmul(bank_c[p:p + KB, EXPERTS:2 * EXPERTS], enc_sb[:, KA:C], switch_in[:, :],
                          start=True, stop=True)
            last = pe.matmul(bank_e[:, 0:EXPERTS], enc_sb[:, C:C + 1].to_broadcast([HID + 1, 128]),
                             switch_in[:, :], start=True, stop=True)
            last.then_inc(s_fold, 1)
            pe.wait_ge(s_folded, 5)
            pe.wait_ge(s_split, len(SPLITS) + 1)

            def passes(act_s, act_g, parts, cols, toks):
                high, mixed, low = (act_s[:, n, toks] for n in range(3))
                if act_g is None:
                    last_act, kg = act_s[KB:128, 1, toks], slice(KB, 128)
                else:
                    last_act, kg = act_g[0:KG, toks], slice(0, KG)
                return [(high, parts[:, 0, cols]), (high, parts[:, 1, cols]), (low, parts[:, 0, cols]),
                        (mixed, parts[:, 2, cols]), (last_act, parts[kg, 3, cols])]

            def token_major(out_ap, *operands):
                five = passes(*operands)
                for n, (a_, w_) in enumerate(five):
                    last = pe.matmul(out_ap, a_, w_, start=(n == 0), stop=(n == len(five) - 1))
                return last

            def feature_major(out_ap, *operands):
                five = passes(*operands)
                for n, (a_, w_) in enumerate(five):
                    last = pe.matmul(out_ap, w_, a_, start=(n == 0), stop=(n == len(five) - 1))
                return last

            def half(t):
                return slice(t * T, (t + 1) * T)

            def split_transposes(bank, src):
                for t in range(2):
                    pe.transpose(bank[:, t * T:(t + 1) * T], src[:, t, 0:KA], ident_sb[0:T, 0:T])
                for t in range(2):
                    last = pe.transpose(bank[:, TOKENS + t * T:TOKENS + (t + 1) * T],
                                        src[:, t, KB:C], ident_sb[0:T, 0:T])
                return last

            def transposes(bank, src):
                for k in range(2):
                    for t in range(2):
                        last = pe.transpose(bank[0:CH, k * TOKENS + t * T:k * TOKENS + (t + 1) * T],
                                            src[:, t, k * CH:(k + 1) * CH], ident_sb[0:T, 0:T])
                return last

            def experts(x_, xp, g):
                t, pair = g // 4, g % 4
                if g >= 2 or old(x_, 1):
                    pe.wait_ge(ve_combined, 8 * x_ + g - 1)
                token_major(bank_x[g % 2][0:T, 0:PAIR], y1_s[xp], y1_g[xp], expert_h,
                            slice(pair * PAIR, (pair + 1) * PAIR), half(t)).then_inc(pe_expert, 1)

            def step(j, par, clip):
                a, l, b, c, x_, n, d, e = (clip(s) for s in "ALBCXNDE")
                bp, cp, xp = ((par + STAGES[s]) % 2 for s in "BCX")
                if b is not None:
                    pe.wait_ge(ve_y0, b + 1)
                    if old(b, 1):
                        pe.wait_ge(ve_h1, b)
                    transposes(bank_b, y0[bp]).then_inc(pe_y0t, 1)
                if c is not None:
                    pe.wait_ge(ve_y1, c + 1)
                    if e is not None and old(e, 1):
                        pe.wait_ge(ac_gelu, 2 * e)
                    split_transposes(bank_c, y1).then_inc(pe_y1t, 1)
                if d is not None:
                    pe.wait_ge(ac_xn, d + 1)
                    if old(d, 1):
                        pe.wait_ge(ve_probs_t, d)
                    split_transposes(bank_d, xn).then_inc(pe_y2t, 1)
                if e is not None:
                    pe.wait_ge(ve_y3, e + 1)
                    if old(e, 1):
                        pe.wait_ge(ve_out, e)
                    split_transposes(bank_e, y3).then_inc(pe_y3t, 1)
                if x_ is not None:
                    experts(x_, xp, 0)
                if l is not None:
                    pe.wait_ge(ac_log, l + 1)
                    for t in range(2):
                        last = pe.matmul(halves(bank_a, T, C)[:, t, :], log_mel[:, t * T:(t + 1) * T],
                                         embed_sb[:, :], start=True, stop=True)
                    last.then_inc(pe_embed, 1)
                if x_ is not None:
                    experts(x_, xp, 1)
                if n is not None:
                    pe.wait_ge(ac_y2, n + 1)
                    if old(n, 2):
                        pe.wait_ge(ve_h3, n - 1)
                    for t in range(2):
                        last = pe.matmul(bank_d2[:, 0:2], mean_w[:, :], clip_sums[:, t, :],
                                         start=(t == 0), stop=(t == 1))
                    last.then_inc(pe_clip, 1)
                if a is not None:
                    half_count = (a // 2 + 1) * 16 if isinstance(a, int) else (a + (2 - par)) * 8
                    pe.wait_ge(s_frames[par], half_count)
                    if old(a, 1):
                        pe.wait_ge(ve_h0, a)
                    for t in range(2):
                        last = pe.transpose(bank_a[0:FRAME, t * T:(t + 1) * T], frame_sb[par][:, t, :],
                                            ident_sb[0:T, 0:T])
                    last.then_inc(pe_frames, 1)
                if c is not None:
                    pe.wait_ge(ve_y1s, c + 1)
                    for t in range(2):
                        last = token_major(bank_c[0:T, t * EXPERTS:(t + 1) * EXPERTS], y1_s[cp], y1_g[cp],
                                           router_h, slice(0, EXPERTS), half(t))
                    last.then_inc(pe_router, 1)
                if e is not None:
                    pe.wait_ge(ve_y3s, e + 1)
                    for t in range(2):
                        last = token_major(bank_e[0:T, t * EXPERTS:(t + 1) * EXPERTS], y3_s, y3_g,
                                           switch_h, slice(0, EXPERTS), half(t))
                    last.then_inc(pe_switch, 1)
                if b is not None:
                    pe.wait_ge(ac_y0t, b + 1)
                    for t in range(2):
                        for k in range(2):
                            last = pe.matmul(bank_b[0:T, t * QUERIES:(t + 1) * QUERIES],
                                             y0_t[:, k, t * T:(t + 1) * T], y0_t[:, k, 0:QUERIES],
                                             start=(k == 0), stop=(k == 1))
                    last.then_inc(pe_scores_b, 1)
                if d is not None:
                    pe.wait_ge(ve_xnt, d + 1)
                    for m in range(2):
                        last = feature_major(halves(bank_d, 128, TOKENS)[:, m, :], xn_s, None, qk_h,
                                             slice(m * 128, (m + 1) * 128), slice(0, TOKENS))
                    last.then_inc(pe_qk, 1)
                if x_ is not None:
                    experts(x_, xp, 2)
                if a is not None:
                    pe.wait_ge(ac_frame_t, a + 1)
                    pe.matmul(bank_a[0:2 * BINS, 0:TOKENS], dft_sb[:, :], frame_t[:, :],
                              start=True, stop=True).then_inc(pe_dft, 1)
                if d is not None:
                    if n is not None:
                        pe.wait_ge(ve_clip_var, n + 1)
                    for t in range(2):
                        last = token_major(halves(bank_d2, T, C)[:, t, :], xn_s, None, wv_h,
                                           slice(0, C), half(t))
                    last.then_inc(pe_values, 1)
                if e is not None:
                    pe.wait_ge(ve_hot, e + 1)
                    for t in range(2):
                        last = pe.transpose(bank_e[0:72, t * T:(t + 1) * T], hot[:, t, 0:72], ident_sb[0:T, 0:T])
                    last.then_inc(pe_hot_t, 1)
                if x_ is not None:
                    experts(x_, xp, 3)
                if d is not None:
                    pe.wait_ge(ve_qk, d + 1)
                    for t in range(2):
                        five = [(qk_th[:, 0, half(t)], xn_s[:, 0, :]), (qk_th[:, 0, half(t)], xn_s[:, 2, :]),
                                (qk_tl[:, 0, half(t)], xn_s[:, 0, :]), (qk_th[:, 1, half(t)], xn_s[:, 1, :]),
                                (qk_tl[KB:128, 1, half(t)], xn_s[KB:128, 1, :])]
                        for i, (q_, k_) in enumerate(five):
                            last = pe.matmul(halves(bank_d, T, TOKENS)[:, t, :], q_, k_,
                                             start=(i == 0), stop=(i == len(five) - 1))
                    last.then_inc(pe_scores_d, 1)
                if b is not None:
                    pe.wait_ge(ac_probs_b, b + 1)
                    for t in range(2):
                        last = pe.matmul(bank_b[0:QUERIES, 0:C + 1], probs_b[:, t, :], y0[bp][:, t, :],
                                         start=(t == 0), stop=(t == 1))
                    last.then_inc(pe_mix_b, 1)
                if x_ is not None:
                    experts(x_, xp, 4)
                if a is not None:
                    pe.wait_ge(ac_power, a + 1)
                    pe.matmul(bank_a[0:MEL, 0:TOKENS], mel_sb[:, :], power[:, :],
                              start=True, stop=True).then_inc(pe_mel, 1)
                for g in range(2):
                    if e is not None:
                        if g == 0:
                            pe.wait_ge(ve_hot_t, e + 1)
                            if c is not None:
                                pe.wait_ge(ve_mix_w, c + 1)
                        else:
                            pe.wait_ge(ve_masked, 2 * e + 1)
                        for m in range(2):
                            u = 2 * g + m
                            last = pe.matmul(halves(bank_e, 128, TOKENS)[:, m, :],
                                             rows_h[:, u * 128:(u + 1) * 128], hot_t[0:EXPERTS, :],
                                             start=True, stop=True)
                        last.then_inc(pe_mask, 1)
                        for m in range(2):
                            u = 2 * g + m
                            last = feature_major(halves(bank_c, 128, TOKENS)[:, m, :], y3_s, y3_g, w1_h,
                                                 slice(u * 128, (u + 1) * 128), slice(0, TOKENS))
                        last.then_inc(pe_hidden, 1)
                    if g == 0 and b is not None:
                        pe.wait_ge(ve_mix_b, b + 1)
                        for i in range(3):
                            kk = QUERIES + (i == 0)
                            last = pe.matmul(bank_b[0:QUERIES, 0:C], mix_b[0:kk, i:C:3],
                                             attn_sb[0:kk, i, :], start=(i == 0), stop=(i == 2))
                        last.then_inc(pe_proj_b, 1)
                    if g == 0 and d is not None:
                        pe.wait_ge(ac_probs_d, 2 * d + 2)
                        for k in range(2):
                            for t in range(2):
                                last = pe.transpose(bank_d[0:T, k * TOKENS + t * T:k * TOKENS + (t + 1) * T],
                                                    probs_d[:, t, k * T:(k + 1) * T], ident_sb[0:T, 0:T])
                        last.then_inc(pe_probs_t, 1)
                    if x_ is not None:
                        experts(x_, xp, 5 + g)
                if d is not None:
                    pe.wait_ge(ve_probs_t, d + 1)
                    pe.wait_ge(ac_values, d + 1)
                    for t in range(2):
                        for k in range(2):
                            last = pe.matmul(halves(bank_d2, T, C)[:, t, :], probs_t[:, k, t * T:(t + 1) * T],
                                             values[:, k, :], start=(k == 0), stop=(k == 1))
                    last.then_inc(pe_mix_d, 1)
                if x_ is not None:
                    experts(x_, xp, 7)
                if e is not None:
                    pe.wait_ge(ve_masked, 2 * e + 2)
                    for t in range(2):
                        for u in range(4):
                            pe.matmul(halves(bank_e, T, C)[:, t, :], act_m[:, u, t * T:(t + 1) * T],
                                      w2_sb[:, u, :], start=(u == 0), stop=False)
                        last = pe.matmul(halves(bank_e, T, C)[:, t, :], hot_t[:, t * T:(t + 1) * T],
                                         b2_h[:, :], start=False, stop=True)
                    last.then_inc(pe_out, 1)

            run(pe, step)

        @block.vector
        def _(dve):
            dve.wait_ge(s_load, LOADED)
            dve.wait_ge(s_ones, 1)

            for g in (y1_g[0], y1_g[1], y3_g):
                dve.memset(g[BIAS_H:BIAS_H + 1, :], 1.0)
                dve.memset(g[BIAS_L:BIAS_L + 1, :], 1.0)
            for n, (full, parts, scale, bias) in enumerate(SPLITS):
                dve.wait_ge(s_high, n + 1)
                dve.scalar_tensor_tensor(parts[:, 1, :], full[:, 0, :], scale, parts[:, 0, :],
                                         ALU.mult, ALU.subtract)
                low = slice(0, KB) if bias else slice(KB, 128)
                last = dve.scalar_tensor_tensor(parts[low, 3, :], full[low, 1, :], scale, parts[low, 2, :],
                                                ALU.mult, ALU.subtract)
                if bias:
                    row = slice(BIAS_L, BIAS_L + 1)
                    last = dve.scalar_tensor_tensor(parts[row, 3, :], full[row, 2, :], scale, parts[row, 3, :],
                                                    ALU.mult, ALU.subtract)
                last.then_inc(s_split, 1)
            dve.wait_ge(s_b2, 16 * len(B2_LOADS))
            left = b2_f
            for i in range(3):
                dve.tensor_copy(b2_part[i][:, :], left[:, :]).then_inc(s_b2, 1)
                dve.wait_ge(s_b2, 16 * len(B2_LOADS) + 2 * i + 1)
                last = dve.tensor_copy(b2_h[32 * i:32 * i + EXPERTS, :], b2_part[i][32 * i:32 * i + EXPERTS, :])
                if i < 2:
                    dve.tensor_tensor(b2_rest[i][:, :], left[:, :], b2_part[i][:, :],
                                      ALU.subtract).then_inc(s_b2, 1)
                    dve.wait_ge(s_b2, 16 * len(B2_LOADS) + 2 * i + 2)
                    left = b2_rest[i]
            last.then_inc(s_split, 1)

            def low_parts(bank, parts):
                dve.tensor_tensor(parts[:, 2, :], bank[:, 0:TOKENS], parts[:, 0, :], ALU.subtract)
                return dve.tensor_tensor(parts[0:KB, 1, :], bank[KB:128, TOKENS:2 * TOKENS],
                                         parts[KB:128, 1, :], ALU.subtract)

            def statistics(k, src, b, own):
                for t in range(2):
                    dve.bn_stats(stats[k][:, t, :], src[:, t, :]).then_inc(ve_own, 1)
                dve.wait_ge(ve_own, own + 2)
                if old(b, 1):
                    dve.wait_ge(po_shift2 if k == 2 else po_rdev[k], b)
                settled(dve)
                for t in range(2):
                    last = dve.bn_aggr(moments[k][:, t, :], stats[k][:, t, :])
                last.then_inc(ve_moments[k], 1)

            def normalize(k, src, dst, b):
                dve.wait_ge(po_rdev[k], b + 1)
                for t in range(2):
                    last = dve.tensor_scalar(dst[:, t, 0:C], src[:, t, :], moments[k][:, t, 0:1],
                                             rdev[k][:, t:t + 1], ALU.subtract, ALU.mult)
                return last

            def combine(x_, xp, g):
                t, pair = g // 4, 2 * (g % 4)
                so_far = h2[xp] if g % 4 else h1[xp]
                dve.wait_ge(pe_expert, 8 * x_ + g + 1)
                if g:
                    dve.wait_ge(ve_combined, 8 * x_ + g)
                dve.scalar_tensor_tensor(h2[xp][:, t, :], bank_x[g % 2][0:T, 0:C],
                                         mix_w[xp][:, t, pair:pair + 1], so_far[:, t, :],
                                         ALU.mult, ALU.add).then_inc(ve_pair, 1)
                dve.wait_ge(ve_pair, 8 * x_ + g + 1)
                dve.scalar_tensor_tensor(h2[xp][:, t, :], bank_x[g % 2][0:T, C:2 * C],
                                         mix_w[xp][:, t, pair + 1:pair + 2], h2[xp][:, t, :],
                                         ALU.mult, ALU.add).then_inc(ve_combined, 1)

            def step(j, par, clip):
                l, b, c, x_, n, d, e = (clip(s) for s in "LBCXNDE")
                lp, bp, cp, xp, dp, ep = ((par + STAGES[s]) % 2 for s in "LBCXDE")
                own = own_before(j)
                if c is not None:
                    dve.wait_ge(ac_y1g, c + 1)
                    low_parts(bank_c, y1_s[cp]).then_inc(ve_y1s, 1)
                if d is not None:
                    dve.wait_ge(ac_xnt, d + 1)
                    low_parts(bank_d, xn_s).then_inc(ve_xnt, 1)
                if e is not None:
                    dve.wait_ge(ac_y3g, e + 1)
                    low_parts(bank_e, y3_s).then_inc(ve_y3s, 1)
                if x_ is not None:
                    dve.wait_ge(po_h1, x_ + 1)
                    dve.wait_ge(ve_h1, x_ + 1)
                    if old(x_, 2):
                        dve.wait_ge(po_h3, x_ - 1)
                    dve.wait_ge(ve_mix_w, x_ + 1)
                    combine(x_, xp, 0)
                if l is not None:
                    dve.wait_ge(pe_embed, l + 1)
                    if old(l, 2):
                        dve.wait_ge(po_h1, l - 1)
                    dve.tensor_copy(h0[lp][:, :, :], halves(bank_a, T, C)).then_inc(ve_h0, 1)
                    dve.wait_ge(ve_h0, l + 1)
                    statistics(0, h0[lp], l, own)
                    own = own + 2
                if x_ is not None:
                    combine(x_, xp, 1)
                if n is not None:
                    dve.wait_ge(pe_clip, n + 1)
                    if old(n, 1):
                        dve.wait_ge(po_clip_rdev, n)
                    dve.tensor_copy(clip_moments[:, :], bank_d2[:, 0:2]).then_inc(ve_own, 1)
                    dve.wait_ge(ve_own, own + 1)
                    dve.tensor_tensor(mean_sq[:, :], clip_moments[:, 0:1], clip_moments[:, 0:1],
                                      ALU.mult).then_inc(ve_own, 1)
                    dve.wait_ge(ve_own, own + 2)
                    dve.tensor_tensor(clip_var[:, :], clip_moments[:, 1:2], mean_sq[:, :],
                                      ALU.subtract).then_inc(ve_clip_var, 1)
                    own = own + 2
                if c is not None:
                    dve.wait_ge(pe_router, c + 1)
                    settled(dve)
                    for t in range(2):
                        dve.max(top[:, t, :], bank_c[0:T, t * EXPERTS:(t + 1) * EXPERTS]).then_inc(ve_own, 1)
                    dve.wait_ge(ve_own, own + 2)
                    dve.tensor_scalar(neg_top[:, :], top[:, :, 0], -1.0 / EXPERT_SCALE, None,
                                      ALU.mult).then_inc(ve_top, 1)
                    for t in range(2):
                        dve.max_index(top_at[:, t, :], top[:, t, :],
                                      bank_c[0:T, t * EXPERTS:(t + 1) * EXPERTS]).then_inc(ve_own, 1)
                    own = own + 4
                if e is not None:
                    dve.wait_ge(pe_switch, e + 1)
                    settled(dve)
                    for t in range(2):
                        dve.max(best[:, t, :], bank_e[0:T, t * EXPERTS:(t + 1) * EXPERTS]).then_inc(ve_own, 1)
                    dve.wait_ge(ve_own, own + 2)
                    dve.tensor_scalar(neg_best[:, :], best[:, :, 0], -1.0, None, ALU.mult).then_inc(ve_best, 1)
                    for t in range(2):
                        dve.max_index(best_at[:, t, :], best[:, t, :],
                                      bank_e[0:T, t * EXPERTS:(t + 1) * EXPERTS]).then_inc(ve_own, 1)
                    own = own + 4
                    dve.wait_ge(ve_own, own)
                    dve.tensor_tensor(hot[:, :, :].rearrange("p t (i n) -> p t i n", i=3)[:, :, :, 0:EXPERTS],
                                      iota_sb[0:T, :].unsqueeze(1).unsqueeze(1).to_broadcast([T, 2, 3, EXPERTS]),
                                      best_at[:, :, 0:1].unsqueeze(3).to_broadcast([T, 2, 3, EXPERTS]),
                                      ALU.is_equal).then_inc(ve_hot, 1)
                if c is not None:
                    dve.wait_ge(ve_own, own)
                    dve.tensor_tensor(pick_hot[:, :, :, :],
                                      iota_sb[0:T, :].unsqueeze(1).unsqueeze(1).to_broadcast([T, 2, 2, EXPERTS]),
                                      top_at[:, :, 0:2].unsqueeze(3).to_broadcast([T, 2, 2, EXPERTS]),
                                      ALU.is_equal).then_inc(ve_own, 1)
                    own = own + 1
                if l is not None:
                    normalize(0, h0[lp], y0[lp], l).then_inc(ve_y0, 1)
                if x_ is not None:
                    combine(x_, xp, 2)
                if d is not None:
                    dve.wait_ge(ac_qk, d + 1)
                    dve.tensor_tensor(qk_tl[:, :, :], halves(bank_d, 128, TOKENS), qk_th[:, :, :],
                                      ALU.subtract).then_inc(ve_qk, 1)
                if e is not None:
                    dve.wait_ge(pe_hot_t, e + 1)
                    dve.tensor_copy(hot_t[:, :], bank_e[0:72, 0:TOKENS]).then_inc(ve_hot_t, 1)
                if c is not None:
                    dve.wait_ge(ac_top_exp, 2 * c + 2)
                    dve.scalar_tensor_tensor(denom[:, :], exp_sum[:, :], 1e-9, top_exp[:, :, 1],
                                             ALU.mult, ALU.add).then_inc(ve_own, 1)
                    dve.wait_ge(ve_own, own + 1)
                    dve.tensor_scalar(denom1[:, :], denom[:, :], 1.0, EXPERT_SCALE, ALU.add,
                                      ALU.mult).then_inc(ve_own, 1)
                    dve.wait_ge(ve_own, own + 2)
                    dve.reciprocal(rdenom[:, :], denom1[:, :]).then_inc(ve_own, 1)
                    dve.wait_ge(ve_own, own + 3)
                    dve.tensor_tensor(pick_w[:, :, :], top_exp[:, :, 0:2],
                                      rdenom[:, :].unsqueeze(2).to_broadcast([T, 2, 2]),
                                      ALU.mult).then_inc(ve_own, 1)
                    dve.wait_ge(ve_own, own + 4)
                    dve.tensor_tensor(pick_mix[:, :, :, :], pick_hot[:, :, :, :],
                                      pick_w[:, :, :].unsqueeze(3).to_broadcast([T, 2, 2, EXPERTS]),
                                      ALU.mult).then_inc(ve_own, 1)
                    dve.wait_ge(ve_own, own + 5)
                    own = own + 5
                    dve.tensor_tensor(mix_w[cp][:, :, :], pick_mix[:, :, 0, :], pick_mix[:, :, 1, :],
                                      ALU.add).then_inc(ve_mix_w, 1)
                if x_ is not None:
                    combine(x_, xp, 3)
                if d is not None:
                    dve.wait_ge(pe_scores_d, d + 1)
                    for t in range(2):
                        last = dve.tensor_reduce(neg_max[:, t:t + 1], bank_d[0:T, t * TOKENS:(t + 1) * TOKENS],
                                                 AX_X, ALU.max, negate=True)
                    last.then_inc(ve_max_d, 1)
                if b is not None:
                    dve.wait_ge(pe_mix_b, b + 1)
                    dve.reciprocal(rsum_b[:, :], bank_b[0:QUERIES, C:C + 1]).then_inc(ve_own, 1)
                    own = own + 1
                    dve.wait_ge(ve_own, own)
                    dve.tensor_scalar(mix_b[0:QUERIES, :], bank_b[0:QUERIES, 0:C], rsum_b[:, :], None,
                                      ALU.mult).then_inc(ve_mix_b, 1)
                if x_ is not None:
                    combine(x_, xp, 4)
                if e is not None:
                    dve.wait_ge(pe_mask, 2 * e + 1)
                    dve.wait_ge(ac_gelu, 2 * e + 1)
                    dve.tensor_tensor(act_m[:, 0:2, :], act_h[:, 0:2, :], halves(bank_e, 128, TOKENS),
                                      ALU.mult).then_inc(ve_masked, 1)
                if b is not None:
                    dve.wait_ge(pe_proj_b, b + 1)
                    dve.wait_ge(po_h1, b + 1)
                    dve.tensor_tensor(h1[bp][0:QUERIES, 0, :], bank_b[0:QUERIES, 0:C], h0[bp][0:QUERIES, 0, :],
                                      ALU.add).then_inc(ve_h1, 1)
                    dve.wait_ge(ve_h1, b + 1)
                    statistics(1, h1[bp], b, own)
                    own = own + 2
                if d is not None:
                    dve.wait_ge(pe_probs_t, d + 1)
                    dve.tensor_copy(probs_t[:, :, :], halves(bank_d, T, TOKENS)).then_inc(ve_probs_t, 1)
                if x_ is not None:
                    combine(x_, xp, 5)
                if b is not None:
                    if old(b, 1):
                        dve.wait_ge(pe_y1t, b)
                    normalize(1, h1[bp], y1, b).then_inc(ve_y1, 1)
                if e is not None:
                    dve.wait_ge(pe_mask, 2 * e + 2)
                    dve.wait_ge(ac_gelu, 2 * e + 2)
                    dve.tensor_tensor(act_m[:, 2:4, :], act_h[:, 2:4, :], halves(bank_e, 128, TOKENS),
                                      ALU.mult).then_inc(ve_masked, 1)
                if x_ is not None:
                    combine(x_, xp, 6)
                if d is not None:
                    dve.wait_ge(ac_probs_d, 2 * d + 2)
                    dve.reciprocal(rsum_d[:, :], sum_d[:, :]).then_inc(ve_own, 1)
                    own = own + 1
                    dve.wait_ge(ve_own, own)
                    dve.wait_ge(pe_mix_d, d + 1)
                    dve.wait_ge(po_h3, d + 1)
                    for t in range(2):
                        last = dve.scalar_tensor_tensor(h3[dp][:, t, :], halves(bank_d2, T, C)[:, t, :],
                                                        rsum_d[:, t:t + 1], h3[dp][:, t, :],
                                                        ALU.mult, ALU.add)
                    last.then_inc(ve_h3, 1)
                    dve.wait_ge(ve_h3, d + 1)
                    statistics(3, h3[dp], d, own)
                    own = own + 2
                if x_ is not None:
                    combine(x_, xp, 7)
                    dve.wait_ge(ve_combined, 8 * x_ + 8)
                    statistics(2, h2[xp], x_, own)
                    own = own + 2
                if d is not None:
                    if old(d, 1):
                        dve.wait_ge(pe_y3t, d)
                    normalize(3, h3[dp], y3, d).then_inc(ve_y3, 1)
                if e is not None:
                    dve.wait_ge(ac_route_exp, 2 * e + 2)
                    dve.reciprocal(route_prob[:, :], route_sum[:, :]).then_inc(ve_own, 1)
                    own = own + 1
                    dve.wait_ge(ve_own, own)
                    dve.wait_ge(pe_out, e + 1)
                    if old(e, 2):
                        stored = (e // 2) * 16 if isinstance(e, int) else (e - ep) * 8
                        dve.wait_ge(s_stored[ep], stored)
                    for t in range(2):
                        last = dve.scalar_tensor_tensor(out_sb[ep][:, t, :], halves(bank_e, T, C)[:, t, :],
                                                        route_prob[:, t:t + 1], h3[ep][:, t, :],
                                                        ALU.mult, ALU.add)
                    last.then_inc(ve_out, 1)

            OWN = {"L": 2, "B": 1 + 2, "C": 4 + 1 + 5, "X": 2, "N": 2, "D": 1 + 2, "E": 4 + 1}

            def own_before(j):
                return before(OWN, j)

            run(dve, step)


def kernel(**inputs):
    import numpy as np
    import concourse.bacc as bacc
    from concourse.bass_utils import run_bass_kernel_spmd

    def rows(*parts):
        return np.concatenate([np.atleast_2d(p) for p in parts], axis=0)

    given = {k: np.asarray(v) for k, v in inputs.items()}
    n = np.arange(FRAME)
    window = (0.54 - 0.46 * np.cos(2.0 * np.pi * n / (FRAME - 1))).astype(np.float32).astype(np.float64)
    angle = 2.0 * np.pi * ((n[:, None] * np.arange(BINS)[None, :]) % FRAME) / FRAME
    dft = np.concatenate([window[:, None] * np.cos(angle), -window[:, None] * np.sin(angle)], axis=1)
    one_hot_row = np.zeros((1, MEL + 1), np.float32)
    one_hot_row[0, MEL] = 1.0
    enc_row = np.zeros((1, C + 1), np.float32)
    enc_row[0, C] = 1.0
    g = given
    arrays = {
        "x": g["x"],
        "dft": dft.astype(np.float32),
        "ident": np.eye(128, dtype=np.float32),
        "iota": np.tile(np.arange(EXPERTS, dtype=np.float32), (128, 1)),
        "expert_rows": np.repeat(np.eye(EXPERTS, dtype=np.float32), HID, axis=1),
        "mel_w": rows(g["L0_tok_mel_filters"].T, g["L0_tok_mel_filters"].T),
        "dct_w": rows(np.concatenate([g["L0_tok_dct"], np.zeros((MFCC, 1), np.float32)], axis=1), one_hot_row),
        "embed_w": rows(g["L0_tok_w_proj"], g["L0_tok_b_proj"]),
        "attn_w": g["L0_attn_proj_w"].T,
        "attn_b": g["L0_attn_proj_b"][None, :],
        "router_w": rows(g["L0_ffn_router_w"].T, g["L0_ffn_router_b"]),
        "expert_w": rows(g["L0_ffn_expert_w"].transpose(2, 0, 1).reshape(C, EXPERTS * C),
                         g["L0_ffn_expert_b"].reshape(1, EXPERTS * C)),
        "wq": g["L1_attn_Wq"],
        "wk": g["L1_attn_Wk"],
        "wv": g["L1_attn_Wv"].T,
        "enc_w": rows(np.concatenate([g["L1_ffn_enc_w"].T, g["L1_ffn_enc_b"][:, None]], axis=1), enc_row),
        "switch_w": rows(g["L1_ffn_sw_w"], g["L1_ffn_sw_b"]),
        "w1": rows(g["L1_ffn_w1"].transpose(1, 0, 2).reshape(C, EXPERTS * HID),
                   g["L1_ffn_b1"].reshape(1, EXPERTS * HID)),
        "w2": g["L1_ffn_w2"].reshape(EXPERTS * HID, C),
        "b2": g["L1_ffn_b2"],
    }
    arrays = {f"in_{k}": np.ascontiguousarray(v) for k, v in arrays.items()}
    nc = bacc.Bacc("TRN2", target_bir_lowering=False, num_devices=1)
    args = [nc.dram_tensor(k, v.shape, mybir.dt.from_np(v.dtype), kind="ExternalInput").ap()
            for k, v in arrays.items()]
    out = nc.dram_tensor("out_0", (CLIPS, TOKENS, C), F32, kind="ExternalOutput").ap()
    tower(nc, *args, out)
    result = run_bass_kernel_spmd(nc, [arrays], core_ids=[0])
    return result.results[0]["out_0"]
```

```python
from contextlib import ExitStack

import concourse.bass as bass
from concourse import mybir

ALU = mybir.AluOpType
ACT = mybir.ActivationFunctionType
F32 = mybir.dt.float32
F16 = mybir.dt.float16
U32 = mybir.dt.uint32
AX_X = mybir.AxisListType.X

CLIPS, AUDIO = 32, 40000
FRAME, HOP = 100, 160
TOKENS = 1 + (AUDIO - FRAME) // HOP
T = TOKENS // 2
BINS = FRAME // 2 + 1
MEL, MFCC = 40, 13
C = 192
CH = C // 2
QUERIES = 64
EXPERTS = 8
HID = 64
EPS = 1e-5
KA = 128
KB = C - KA
BIAS_L, BIAS_H = 64, 96
KG = BIAS_H + 1
MASK = BIAS_H + 1
KM = MASK + EXPERTS
LOW_MEL = 64
KE = LOW_MEL + MEL
KB2 = 32 + 8
EXPERT_SCALE = 64.0
HIDDEN_SCALE = 16.0
OUT_SCALE = 64.0
MASK_W, MASK_X = 32768.0, 32768.0
VALUE_SCALE = 64.0
EMBED_SCALE = 64.0
PAIR = 2 * C

STAGES = {"A": 0, "L": 0, "B": 1, "C": 2, "X": 2, "N": 3, "D": 4, "E": 5, "O": 6}
LAST = STAGES["O"]
FIRST_LOOPED = 8
END_LOOPED = CLIPS


def tower(nc, x, dft, ident, iota, mel_w, dct_w, embed_w, attn_w, router_w, expert_w, wq, wk, wv,
          enc_w, switch_w, w1, w2, b2, out):
    frames = x.rearrange("b (t p n) -> b p t n", t=2, n=HOP)
    out_tokens = out.rearrange("b (t p) c -> b p t c", t=2)

    with ExitStack() as ctx:
        def sb(name, shape, dt=F32):
            return ctx.enter_context(nc.sbuf_tensor(name, shape, dt))

        def ps(name, shape, dt=F32):
            return ctx.enter_context(nc.psum_tensor(name, shape, dt))

        def sem(name):
            return ctx.enter_context(nc.semaphore(name))

        dft_sb = sb("dft_sb", [FRAME, 2 * BINS])
        ident_sb = sb("ident_sb", [128, 128])
        iota_sb = sb("iota_sb", [128, EXPERTS])
        mel_sb = sb("mel_sb", [2 * BINS, MEL])
        dct_sb = sb("dct_sb", [MFCC + 1, MEL + 1])
        embed_in = sb("embed_in", [MFCC + 1, C])
        embed_h = sb("embed_h", [KE, 2, C], F16)
        attn_sb = sb("attn_sb", [128, 2, C])
        router_f = sb("router_f", [128, 2, EXPERTS])
        router_h = sb("router_h", [128, 4, EXPERTS], F16)
        expert_f = sb("expert_f", [128, 2, EXPERTS * C])
        expert_h = sb("expert_h", [128, 4, EXPERTS * C], F16)
        w1_f = sb("w1_f", [128, 2, EXPERTS * HID])
        w1_h = sb("w1_h", [128, 4, EXPERTS * HID], F16)
        wv_f = sb("wv_f", [128, 2, C])
        wv_h = sb("wv_h", [128, 4, C], F16)
        qk_f = sb("qk_f", [128, 2, 256])
        qk_h = sb("qk_h", [128, 4, 256], F16)
        switch_f = sb("switch_f", [128, 2, EXPERTS])
        switch_h = sb("switch_h", [128, 4, EXPERTS], F16)
        wq_sb = sb("wq_sb", [CH, 2, C])
        wk_sb = sb("wk_sb", [CH, 2, C])
        enc_sb = sb("enc_sb", [HID + 1, C + 1])
        switch_in = sb("switch_in", [HID + 1, EXPERTS])
        w2_sb = sb("w2_sb", [128, 4, C])
        w2_h = sb("w2_h", [128, 4, C], F16)
        w2_l = sb("w2_l", [128, 4, C], F16)
        b2_f = sb("b2_f", [KB2, C])
        b2_h = sb("b2_h", [KB2, C], F16)
        mean_w = sb("mean_w", [T, 128])
        log_eps = sb("log_eps", [128, 1])
        minus_half = sb("minus_half", [128, 2])

        frame_sb = [sb(f"frame_sb{i}", [T, 2, FRAME]) for i in range(2)]
        frame_t = sb("frame_t", [FRAME, TOKENS])
        power = sb("power", [2 * BINS, TOKENS])
        log_mel = sb("log_mel", [MEL, TOKENS])
        log_s = sb("log_s", [KE, TOKENS], F16)
        h0 = [sb(f"h0_{i}", [T, 2, C]) for i in range(2)]
        stats = [sb(f"stats{k}", [T, 2, 6]) for k in range(4)]
        moments = [sb(f"moments{k}", [T, 2, 2]) for k in range(4)]
        var_eps = [sb(f"var_eps{k}", [T, 2]) for k in range(4)]
        rdev = [sb(f"rdev{k}", [T, 2]) for k in range(4)]
        y0 = [sb(f"y0_{i}", [T, 2, C + 1]) for i in range(2)]
        y0_t = sb("y0_t", [CH, 2, TOKENS])
        probs_b = sb("probs_b", [T, 2, 2, QUERIES])
        rsum_b = sb("rsum_b", [128, 1])
        mix_b = sb("mix_b", [128, 2, QUERIES])
        h1 = [sb(f"h1_{i}", [T, 2, C]) for i in range(2)]
        y1 = sb("y1", [T, 2, C])
        y1_s = [sb(f"y1_s{i}", [128, 3, TOKENS], F16) for i in range(2)]
        y1_g = [sb(f"y1_g{i}", [128, TOKENS], F16) for i in range(2)]
        top = sb("top", [T, 2, 8])
        top_at = sb("top_at", [T, 2, 8], U32)
        neg_top = sb("neg_top", [T, 2])
        top_exp = sb("top_exp", [T, 2, 8])
        exp_sum = sb("exp_sum", [T, 2])
        denom = sb("denom", [T, 2])
        denom1 = sb("denom1", [T, 2])
        rdenom = sb("rdenom", [T, 2])
        pick_w = sb("pick_w", [T, 2, 2])
        pick_hot = sb("pick_hot", [T, 2, 2, EXPERTS])
        pick_mix = sb("pick_mix", [T, 2, 2, EXPERTS])
        mix_w = [sb(f"mix_w{i}", [T, 2, EXPERTS]) for i in range(2)]
        h2 = [sb(f"h2_{i}", [T, 2, C]) for i in range(2)]
        shift = {k: sb(f"shift{k}", [T, 2]) for k in (0, 2)}
        y2 = sb("y2", [T, 2, C])
        y2_sq = sb("y2_sq", [T, 2, C])
        clip_sums = sb("clip_sums", [T, 2, 2])
        clip_moments = sb("clip_moments", [128, 2])
        mean_sq = sb("mean_sq", [128, 1])
        clip_var = sb("clip_var", [128, 1])
        clip_var_eps = sb("clip_var_eps", [128, 1])
        clip_rdev = sb("clip_rdev", [128, 1])
        clip_mean = sb("clip_mean", [128, 1])
        clip_shift = sb("clip_shift", [128, 1])
        xn = sb("xn", [T, 2, C])
        xn_s = sb("xn_s", [128, 3, TOKENS], F16)
        qk_th = sb("qk_th", [128, 2, TOKENS], F16)
        qk_tl = sb("qk_tl", [128, 2, TOKENS], F16)
        values_h = sb("values_h", [T, 2, C], F16)
        values_l = sb("values_l", [T, 2, C], F16)
        neg_max = sb("neg_max", [T, 2])
        probs_d = sb("probs_d", [T, 2, TOKENS])
        probs_th = sb("probs_th", [T, 2, TOKENS], F16)
        probs_tl = sb("probs_tl", [T, 2, TOKENS], F16)
        sum_d = sb("sum_d", [T, 2])
        rsum_d = sb("rsum_d", [T, 2])
        h3 = [sb(f"h3_{i}", [T, 2, C]) for i in range(2)]
        y3 = sb("y3", [T, 2, C])
        y3_s = sb("y3_s", [128, 3, TOKENS], F16)
        y3_g = sb("y3_g", [128, TOKENS], F16)
        best = sb("best", [T, 2, 8])
        best_at = sb("best_at", [T, 2, 8], U32)
        neg_best = sb("neg_best", [T, 2])
        route_exp = sb("route_exp", [T, 2, 8])
        route_sum = sb("route_sum", [T, 2])
        route_prob = sb("route_prob", [T, 2])
        hot = sb("hot", [T, 2, KM])
        hot_t = sb("hot_t", [KB2, TOKENS], F16)
        mask_scale = sb("mask_scale", [128, 1])
        route_scaled = sb("route_scaled", [T, 2])
        units = sb("units", [128, 4, TOKENS])
        units_h = sb("units_h", [128, 4, TOKENS], F16)
        units_l = sb("units_l", [128, 4, TOKENS], F16)
        out_sb = [sb(f"out_sb{i}", [T, 2, C]) for i in range(2)]

        bank_a = ps("bank_a", [128, 512])
        bank_b = ps("bank_b", [128, 512])
        bank_c = ps("bank_c", [128, 512])
        bank_d = ps("bank_d", [128, 512])
        bank_d2 = ps("bank_d2", [128, 512])
        bank_e = ps("bank_e", [128, 512])
        bank_x = [ps(f"bank_x{i}", [128, 512]) for i in range(2)]

        def halves(bank, rows, n):
            return bank[0:rows, 0:2 * n].rearrange("p (t n) -> p t n", t=2)

        s_load = {g: sem(f"s_load_{g}") for g in ("front", "attention", "experts", "values", "switch")}
        s_ones = sem("s_ones")
        s_high = sem("s_high")
        s_split = sem("s_split")
        s_fold = sem("s_fold")
        s_folded = sem("s_folded")
        s_embed = sem("s_embed")
        s_frames = [sem(f"s_frames{i}") for i in range(2)]
        s_stored = [sem(f"s_stored{i}") for i in range(2)]
        pe_frames, pe_dft, pe_mel, pe_embed = (sem(n) for n in ("pe_frames", "pe_dft", "pe_mel", "pe_embed"))
        pe_y0t, pe_scores_b, pe_mix_b, pe_proj_b = (sem(n) for n in ("pe_y0t", "pe_scores_b", "pe_mix_b", "pe_proj_b"))
        pe_y1t, pe_router, pe_expert = (sem(n) for n in ("pe_y1t", "pe_router", "pe_expert"))
        pe_clip, pe_y2t, pe_qk, pe_values, pe_scores_d, pe_probs_t, pe_mix_d = (
            sem(n) for n in ("pe_clip", "pe_y2t", "pe_qk", "pe_values", "pe_scores_d", "pe_probs_t", "pe_mix_d"))
        pe_y3t, pe_switch, pe_hot_t, pe_hidden, pe_out = (
            sem(n) for n in ("pe_y3t", "pe_switch", "pe_hot_t", "pe_hidden", "pe_out"))
        ac_frame_t, ac_power, ac_log, ac_y0t, ac_probs_b, ac_y1g, ac_top_exp = (
            sem(n) for n in ("ac_frame_t", "ac_power", "ac_log", "ac_y0t", "ac_probs_b", "ac_y1g", "ac_top_exp"))
        ac_y2, ac_xn, ac_xnt, ac_qk, ac_values, ac_probs_d, ac_probs_t = (
            sem(n) for n in ("ac_y2", "ac_xn", "ac_xnt", "ac_qk", "ac_values", "ac_probs_d", "ac_probs_t"))
        ac_h0, ac_y0, ac_y3g, ac_route_exp, ac_mask, ac_hot_t, ac_gelu = (
            sem(n) for n in ("ac_h0", "ac_y0", "ac_y3g", "ac_route_exp", "ac_mask", "ac_hot_t", "ac_gelu"))
        ve_mix_b, ve_h1, ve_y1, ve_top, ve_pick, ve_weigh, ve_mix_w, ve_pair, ve_combined = (
            sem(n) for n in ("ve_mix_b", "ve_h1", "ve_y1", "ve_top", "ve_pick", "ve_weigh", "ve_mix_w",
                             "ve_pair", "ve_combined"))
        ve_log, ve_y1s, ve_y3s, ve_qk = (sem(n) for n in ("ve_log", "ve_y1s", "ve_y3s", "ve_qk"))
        ve_clip_var, ve_xnt, ve_values, ve_max_d, ve_probs_t = (
            sem(n) for n in ("ve_clip_var", "ve_xnt", "ve_values", "ve_max_d", "ve_probs_t"))
        ve_h3, ve_y3, ve_best, ve_hot, ve_out = (
            sem(n) for n in ("ve_h3", "ve_y3", "ve_best", "ve_hot", "ve_out"))
        ve_moments = [sem(f"ve_moments{k}") for k in range(4)]
        ve_own = sem("ve_own")
        po_shift = {k: sem(f"po_shift{k}") for k in (0, 2)}
        po_rdev = [sem(f"po_rdev{k}") for k in range(4)]
        po_h1, po_h3, po_clip_rdev, po_units, po_own = (
            sem(n) for n in ("po_h1", "po_h3", "po_clip_rdev", "po_units", "po_own"))

        block = ctx.enter_context(nc.Block())

        def run(eng, step):
            def at(j):
                def clip(stage):
                    b = j - STAGES[stage]
                    return b if 0 <= b < CLIPS else None
                step(j, j % 2, clip)

            for j in range(FIRST_LOOPED):
                at(j)
            with eng.Fori(FIRST_LOOPED, END_LOOPED - 1, 2) as i:
                for par in range(2):
                    step(i + par, par, lambda stage, par=par: i + (par - STAGES[stage]))
            for j in range(END_LOOPED, CLIPS + LAST):
                at(j)

        def settled(eng):
            eng.nop(nofuse=True)

        def before(counts, j):
            if isinstance(j, int):
                return sum(n * min(max(j - STAGES[s], 0), CLIPS) for s, n in counts.items())
            return j * sum(counts.values()) - sum(n * STAGES[s] for s, n in counts.items())

        def old(b, back):
            return not isinstance(b, int) or b >= back

        def first(j, n):
            return isinstance(j, int) and j == n

        def weights(dst, src, bias=None):
            if bias is None:
                return [(dst[:, :, :], src.rearrange("(t p) n -> p t n", t=2))]
            return [(dst[:, 0, :], src[0:KA, :]), (dst[0:bias, 1, :], src[KA:KA + bias, :])]

        LOADS = {
            "front": [(ident_sb[:, :], ident), (dft_sb[:, :], dft), (mel_sb[:, :], mel_w),
                      (dct_sb[:, :], dct_w), (embed_in[:, :], embed_w)],
            "attention": [(iota_sb[:, :], iota), (attn_sb[:, 0, :], attn_w[0:128, :]),
                          (attn_sb[0:QUERIES + 1, 1, :], attn_w[128:C + 1, :]),
                          (enc_sb[:, :], enc_w), (switch_in[:, :], switch_w),
                          (wq_sb[:, :, :], wq.rearrange("(t p) n -> p t n", t=2)),
                          (wk_sb[:, :, :], wk.rearrange("(t p) n -> p t n", t=2))],
            "experts": weights(router_f, router_w, KG) + weights(expert_f, expert_w, KG),
            "values": weights(wv_f, wv),
            "switch": weights(w1_f, w1, KM) + [(w2_sb[:, :, :], w2.rearrange("(t p) n -> p t n", t=4)),
                                               (b2_f[:, :], b2)],
        }
        LOADED = {g: 16 * len(loads) for g, loads in LOADS.items()}
        SPLITS = {1: [(router_f, router_h, EXPERT_SCALE, True, "experts"),
                      (expert_f, expert_h, EXPERT_SCALE, True, "experts")],
                  2: [(wv_f, wv_h, VALUE_SCALE, False, "values"), (qk_f, qk_h, 1.0, False, "attention")],
                  3: [(switch_f, switch_h, 1.0, True, "attention"), (w1_f, w1_h, HIDDEN_SCALE, True, "switch")]}
        OUT_WEIGHTS = 3
        MADE = {"C": 1, "X": 2, "D": 4, "E": 7}

        @block.sync
        def _(sp):
            for dst, src in LOADS["front"]:
                sp.dma_start(dst, src).then_inc(s_load["front"], 16)

            def step(j, par, clip):
                a, e = clip("A"), clip("O")
                if a is not None:
                    if old(a, 2):
                        sp.wait_ge(pe_frames, a - 1)
                    src = frames[a] if isinstance(a, int) else frames[bass.ds(a, 1)].rearrange(
                        "a p t n -> (a p) t n")
                    sp.dma_start(frame_sb[par][:, :, :], src[:, :, 0:FRAME]).then_inc(s_frames[par], 16)
                if first(j, 1):
                    for group in ("attention", "experts", "values", "switch"):
                        for dst, src in LOADS[group]:
                            sp.dma_start(dst, src).then_inc(s_load[group], 16)
                if e is not None:
                    sp.wait_ge(ve_out, e + 1)
                    dst = out_tokens[e] if isinstance(e, int) else out_tokens[bass.ds(e, 1)].rearrange(
                        "a p t c -> (a p) t c")
                    ep = (par + STAGES["O"]) % 2
                    sp.dma_start(dst, out_sb[ep][:, :, :]).then_inc(s_stored[ep], 16)

            run(sp, step)
            for i in range(2):
                sp.wait_ge(s_stored[i], 16 * (CLIPS // 2))

        @block.gpsimd
        def _(pool):
            pool.memset(log_eps[:, :], 1e-6)
            pool.memset(minus_half[:, :], -0.5)
            pool.memset(mean_w[:, :], 1.0 / (TOKENS * C))
            pool.memset(embed_h[:, :, :], 0.0)
            pool.memset(log_s[:, :], 1.0)
            pool.memset(mix_b[:, :, :], 1.0)
            pool.memset(probs_b[:, :, :, :], 0.0)
            pool.memset(b2_h[:, :], 0.0)
            pool.memset(hot[:, :, :], 0.0)
            pool.memset(mask_scale[:, :], MASK_X)
            pool.memset(switch_f[:, 1, :], 0.0)
            for i in range(2):
                pool.memset(y0[i][:, :, :], 1.0)
            for g in (y1_g[0], y1_g[1], y3_g):
                pool.memset(g[:, :], 0.0)
            pool.memset(neg_top[:, :], 0.0).then_inc(s_ones, 1)
            pool.wait_ge(s_ones, 1)

            def layernorm(k, b):
                pool.wait_ge(ve_moments[k], b + 1)
                settled(pool)
                pool.tensor_scalar(var_eps[k][:, :], moments[k][:, :, 1], EPS, None,
                                   ALU.add).then_inc(po_own, 1)

            def power_minus_half(k):
                pool.tensor_tensor(rdev[k][:, :], var_eps[k][:, :], minus_half[0:T, :],
                                   ALU.pow).then_inc(po_rdev[k], 1)

            def one_pass_layernorm(k, b, own):
                layernorm(k, b)
                pool.wait_ge(po_own, own + 1)
                power_minus_half(k)
                pool.wait_ge(po_rdev[k], b + 1)
                pool.tensor_tensor(shift[k][:, :], moments[k][:, :, 0], rdev[k][:, :],
                                   ALU.mult).then_inc(po_own, 1)
                pool.wait_ge(po_own, own + 2)
                settled(pool)
                pool.tensor_scalar(shift[k][:, :], shift[k][:, :], -1.0, None, ALU.mult).then_inc(po_shift[k], 1)
                return own + 2

            def step(j, par, clip):
                l, b, x_, n, d, e = (clip(s) for s in "LBXNDE")
                bp, dp = ((par + STAGES[s]) % 2 for s in "BD")
                own = pool_own_before(j)
                if d is not None:
                    pool.wait_ge(ve_combined, 8 * d + 8)
                    if old(d, 2):
                        pool.wait_ge(ve_out, d - 1)
                    settled(pool)
                    pool.tensor_copy(h3[dp][:, :, :], h2[dp][:, :, :]).then_inc(po_h3, 1)
                if b is not None:
                    pool.wait_ge(ac_y0, b + 1)
                    if old(b, 2):
                        pool.wait_ge(ve_pair, 8 * b - 14)
                        pool.wait_ge(ve_y1, b - 1)
                    pool.tensor_tensor(h1[bp][:, :, :], h0[bp][:, :, :], y0[bp][:, :, 0:C],
                                       ALU.add).then_inc(po_h1, 1)
                if l is not None:
                    if old(l, 1):
                        pool.wait_ge(ac_y0, l)
                    own = one_pass_layernorm(0, l, own)
                if n is not None:
                    pool.wait_ge(ve_clip_var, n + 1)
                    if old(n, 1):
                        pool.wait_ge(ac_xn, n)
                    settled(pool)
                    pool.tensor_scalar(clip_var_eps[:, :], clip_var[:, :], EPS, None,
                                       ALU.add).then_inc(po_own, 1)
                    pool.wait_ge(po_own, own + 1)
                    pool.tensor_tensor(clip_rdev[:, :], clip_var_eps[:, :], minus_half[:, 0:1],
                                       ALU.pow).then_inc(po_own, 1)
                    pool.wait_ge(po_own, own + 2)
                    pool.tensor_tensor(clip_mean[:, :], clip_moments[:, 0:1], clip_rdev[:, :],
                                       ALU.mult).then_inc(po_own, 1)
                    own = own + 3
                    pool.wait_ge(po_own, own)
                    settled(pool)
                    pool.tensor_scalar(clip_shift[:, :], clip_mean[:, :], -1.0, None,
                                       ALU.mult).then_inc(po_clip_rdev, 1)
                if b is not None:
                    layernorm(1, b)
                    own = own + 1
                    pool.wait_ge(po_own, own)
                    power_minus_half(1)
                if e is not None:
                    if old(e, 1):
                        pool.wait_ge(pe_out, e)
                    pool.wait_ge(ac_gelu, 2 * e + 1)
                    pool.tensor_tensor(units_l[:, 0:2, :], units[:, 0:2, :],
                                       units_h[:, 0:2, :], ALU.subtract).then_inc(po_units, 1)
                    pool.wait_ge(ac_gelu, 2 * e + 2)
                    pool.tensor_tensor(units_l[:, 2:4, :], units[:, 2:4, :],
                                       units_h[:, 2:4, :], ALU.subtract).then_inc(po_units, 1)
                if d is not None:
                    layernorm(3, d)
                    own = own + 1
                    pool.wait_ge(po_own, own)
                    power_minus_half(3)
                if x_ is not None:
                    if old(x_, 1):
                        pool.wait_ge(ac_y2, x_)
                    own = one_pass_layernorm(2, x_, own)

            OWN = {"L": 2, "B": 1, "N": 3, "D": 1, "X": 2}

            def pool_own_before(j):
                return before(OWN, j)

            run(pool, step)

        @block.scalar
        def _(act):
            def high_parts(full, parts, scale, bias, group):
                act.wait_ge(s_load[group], LOADED[group])
                act.activation(parts[:, 0, :], full[:, 0, :], ACT.Copy, scale=scale)
                if bias:
                    for p in (0, KB):
                        act.activation(parts[p:p + KB, 2, :], full[0:KB, 1, :], ACT.Copy, scale=scale)
                    k = KM if full is w1_f else KG
                    last = act.activation(parts[0:k, 3, :], full[0:k, 1, :], ACT.Copy, scale=scale)
                else:
                    last = act.activation(parts[:, 2, :], full[:, 1, :], ACT.Copy, scale=scale)
                last.then_inc(s_high, 1)

            def step(j, par, clip):
                a, l, b, c, x_, n, d, e = (clip(s) for s in "ALBCXNDE")
                lp, cp, np_ = ((par + STAGES[s]) % 2 for s in "LCN")
                if first(j, 0):
                    act.wait_ge(s_fold, 1)
                    act.wait_ge(s_ones, 1)
                    act.activation(embed_h[0:MEL + 1, 0, :], bank_b[0:MEL + 1, 0:C], ACT.Copy, scale=EMBED_SCALE)
                    act.activation(embed_h[LOW_MEL:KE, 0, :], bank_b[0:MEL, 0:C], ACT.Copy,
                                   scale=EMBED_SCALE).then_inc(s_folded, 1)
                if a is not None:
                    act.wait_ge(pe_frames, a + 1)
                    act.activation(frame_t[:, :], bank_a[0:FRAME, 0:TOKENS], ACT.Copy).then_inc(ac_frame_t, 1)
                if d is not None:
                    act.wait_ge(pe_y2t, d + 1)
                    act.activation(xn_s[:, 0:2, :], halves(bank_d, 128, TOKENS), ACT.Copy).then_inc(ac_xnt, 1)
                if b is not None:
                    act.wait_ge(pe_y0t, b + 1)
                    act.activation(y0_t[:, :, :], halves(bank_b, CH, TOKENS), ACT.Copy).then_inc(ac_y0t, 1)
                if c is not None:
                    act.wait_ge(pe_y1t, c + 1)
                    if old(c, 2):
                        act.wait_ge(pe_expert, 8 * (c - 1))
                    act.activation(y1_s[cp][:, 0:2, :], halves(bank_c, 128, TOKENS), ACT.Copy)
                    act.activation(y1_g[cp][0:KB, :], bank_c[KB:128, TOKENS:2 * TOKENS],
                                   ACT.Copy).then_inc(ac_y1g, 1)
                if a is not None:
                    act.wait_ge(pe_dft, a + 1)
                    act.activation(power[:, :], bank_a[0:2 * BINS, 0:TOKENS], ACT.Square).then_inc(ac_power, 1)
                if b is not None:
                    act.wait_ge(pe_scores_b, b + 1)
                    act.activation(probs_b[QUERIES:T, 0, :, :],
                                   bank_b[QUERIES:T, 0:QUERIES].unsqueeze(1).to_broadcast([T - QUERIES, 2, QUERIES]),
                                   ACT.Exp, scale=0.25)
                    act.activation(probs_b[:, 1, :, :],
                                   bank_b[0:T, QUERIES:2 * QUERIES].unsqueeze(1).to_broadcast([T, 2, QUERIES]),
                                   ACT.Exp, scale=0.25).then_inc(ac_probs_b, 1)
                if l is not None:
                    act.wait_ge(pe_mel, l + 1)
                    if old(l, 1):
                        act.wait_ge(ve_log, l)
                        act.wait_ge(pe_embed, l)
                    for dst in (log_mel[:, :], log_s[0:MEL, :]):
                        last = act.activation(dst, bank_a[0:MEL, 0:TOKENS], ACT.Ln, bias=log_eps[0:MEL, :])
                    last.then_inc(ac_log, 1)
                if d is not None:
                    act.wait_ge(pe_qk, d + 1)
                    act.activation(qk_th[:, :, :], halves(bank_d, 128, TOKENS), ACT.Copy).then_inc(ac_qk, 1)
                if c is not None:
                    act.wait_ge(ve_top, c + 1)
                    for t in range(2):
                        act.activation(top_exp[:, t, :], top[:, t, :], ACT.Exp, bias=neg_top[:, t:t + 1],
                                       scale=1.0 / EXPERT_SCALE, accum_out=exp_sum[:, t:t + 1]).then_inc(ac_top_exp, 1)
                if e is not None:
                    act.wait_ge(pe_y3t, e + 1)
                    act.activation(y3_s[:, 0:2, :], halves(bank_e, 128, TOKENS), ACT.Copy)
                    act.activation(y3_g[0:KB, :], bank_e[KB:128, TOKENS:2 * TOKENS], ACT.Copy).then_inc(ac_y3g, 1)
                if n is not None:
                    act.wait_ge(ve_combined, 8 * n + 8)
                    act.wait_ge(po_shift[2], n + 1)
                    if old(n, 1):
                        act.wait_ge(pe_clip, n)
                    for t in range(2):
                        act.activation(y2[:, t, :], h2[np_][:, t, :], ACT.Identity, scale=rdev[2][:, t:t + 1],
                                       bias=shift[2][:, t:t + 1], accum_out=clip_sums[:, t, 0:1])
                        last = act.activation(y2_sq[:, t, :], h2[np_][:, t, :], ACT.Square,
                                              scale=rdev[2][:, t:t + 1], bias=shift[2][:, t:t + 1],
                                              accum_out=clip_sums[:, t, 1:2])
                    last.then_inc(ac_y2, 1)
                if l is not None:
                    act.wait_ge(pe_embed, l + 1)
                    if old(l, 2):
                        act.wait_ge(po_h1, l - 1)
                        act.wait_ge(ve_h1, l - 1)
                    act.activation(h0[lp][:, :, :], halves(bank_a, T, C), ACT.Copy,
                                   scale=1.0 / EMBED_SCALE).then_inc(ac_h0, 1)
                if d is not None:
                    act.wait_ge(ve_max_d, d + 1)
                    if old(d, 1):
                        act.wait_ge(ve_h3, d)
                    for t in range(2):
                        act.activation(probs_d[:, t, :], bank_d[0:T, t * TOKENS:(t + 1) * TOKENS], ACT.Exp,
                                       bias=neg_max[:, t:t + 1],
                                       accum_out=sum_d[:, t:t + 1]).then_inc(ac_probs_d, 1)
                    act.wait_ge(pe_values, d + 1)
                    act.activation(values_h[:, :, :], halves(bank_d2, T, C), ACT.Copy,
                                   scale=1.0 / VALUE_SCALE).then_inc(ac_values, 1)
                if e is not None:
                    act.wait_ge(pe_hot_t, e + 1)
                    act.activation(y3_g[BIAS_H:KM, :], bank_e[BIAS_H:KM, 0:TOKENS],
                                   ACT.Identity, scale=mask_scale[BIAS_H:KM, :]).then_inc(ac_mask, 1)
                    if old(e, 1):
                        act.wait_ge(pe_out, e)
                    act.activation(hot_t[:, :], bank_e[0:KB2, 0:TOKENS], ACT.Copy).then_inc(ac_hot_t, 1)
                    act.preload_act_table(ACT.Gelu)
                    if old(e, 1):
                        act.wait_ge(po_units, 2 * e)
                        act.wait_ge(pe_out, e)
                    act.wait_ge(pe_hidden, 2 * e + 1)
                    for dst in (units, units_h):
                        last = act.activation(dst[:, 0:2, :], halves(bank_c, 128, TOKENS),
                                              ACT.Gelu, scale=1.0 / HIDDEN_SCALE)
                    last.then_inc(ac_gelu, 1)
                if d is not None:
                    act.wait_ge(pe_probs_t, d + 1)
                    act.activation(probs_th[:, :, :], halves(bank_d, T, TOKENS), ACT.Copy).then_inc(ac_probs_t, 1)
                if l is not None:
                    act.wait_ge(po_shift[0], l + 1)
                    for t in range(2):
                        last = act.activation(y0[lp][:, t, 0:C], h0[lp][:, t, :], ACT.Identity,
                                              scale=rdev[0][:, t:t + 1], bias=shift[0][:, t:t + 1])
                    last.then_inc(ac_y0, 1)
                if n is not None:
                    act.wait_ge(po_clip_rdev, n + 1)
                    if old(n, 1):
                        act.wait_ge(pe_y2t, n)
                    for t in range(2):
                        last = act.activation(xn[:, t, :], y2[:, t, :], ACT.Identity, scale=clip_rdev[0:T, :],
                                              bias=clip_shift[0:T, :])
                    last.then_inc(ac_xn, 1)
                if e is not None:
                    act.wait_ge(pe_hidden, 2 * e + 2)
                    for dst in (units, units_h):
                        last = act.activation(dst[:, 2:4, :], halves(bank_c, 128, TOKENS),
                                              ACT.Gelu, scale=1.0 / HIDDEN_SCALE)
                    last.then_inc(ac_gelu, 1)
                if e is not None or first(j, 0):
                    act.preload_act_table_set("natural_log_exp_and_others")
                if e is not None:
                    act.wait_ge(ve_best, e + 1)
                    for t in range(2):
                        act.activation(route_exp[:, t, :], best[:, t, :], ACT.Exp, bias=neg_best[:, t:t + 1],
                                       accum_out=route_sum[:, t:t + 1]).then_inc(ac_route_exp, 1)
                if isinstance(j, int) and j in SPLITS:
                    act.wait_ge(s_folded, 2)
                    for split in SPLITS[j]:
                        high_parts(*split)
                if first(j, OUT_WEIGHTS):
                    act.activation(w2_h[:, :, :], w2_sb[:, :, :], ACT.Copy, scale=OUT_SCALE)
                    for p in (0, 32):
                        last = act.activation(b2_h[p:p + EXPERTS, :], b2_f[p:p + EXPERTS, :], ACT.Copy,
                                              scale=OUT_SCALE)
                    last.then_inc(s_high, 1)
                if first(j, 0):
                    act.wait_ge(s_fold, 2)
                    for n_, bank in ((0, bank_b), (1, bank_d)):
                        act.activation(qk_f[:, n_, 0:C], bank[:, 0:C], ACT.Copy)
                        act.activation(qk_f[:, n_, C:256], bank[:, KA:C], ACT.Copy)
                    act.activation(switch_f[:, 0, :], bank_c[:, 0:EXPERTS], ACT.Copy)
                    act.activation(switch_f[0:KB, 1, :], bank_c[0:KB, EXPERTS:2 * EXPERTS], ACT.Copy)
                    for p in (BIAS_L, BIAS_H):
                        last = act.activation(switch_f[p:p + 1, 1, :], bank_e[p:p + 1, 0:EXPERTS], ACT.Copy)
                    last.then_inc(s_folded, 1)

            run(act, step)

        @block.tensor
        def _(pe):
            def fold_embedding():
                pe.matmul(bank_b[0:MEL + 1, 0:C], dct_sb[:, :], embed_in[:, :], start=True,
                          stop=True).then_inc(s_fold, 1)

            def fold_attention_and_switch():
                for bank, m0, m1 in ((bank_b, 0, KA), (bank_d, KA, C)):
                    for p in range(0, 128, m1 - m0):
                        for k in range(2):
                            pe.matmul(bank[p:p + m1 - m0, 0:C], wq_sb[:, k, m0:m1], wk_sb[:, k, :],
                                      start=(k == 0), stop=(k == 1))
                pe.matmul(bank_c[:, 0:EXPERTS], enc_sb[:, 0:KA], switch_in[:, :], start=True, stop=True)
                pe.matmul(bank_c[0:KB, EXPERTS:2 * EXPERTS], enc_sb[:, KA:C], switch_in[:, :],
                          start=True, stop=True)
                pe.matmul(bank_e[:, 0:EXPERTS], enc_sb[:, C:C + 1].to_broadcast([HID + 1, 128]),
                          switch_in[:, :], start=True, stop=True).then_inc(s_fold, 1)

            def passes(act_s, act_g, parts, cols, toks):
                high, mixed, low = (act_s[:, n, toks] for n in range(3))
                if act_g is None:
                    last_act, kg = act_s[KB:128, 1, toks], slice(KB, 128)
                else:
                    kg = slice(0, KM if parts is w1_h else KG)
                    last_act = act_g[kg, toks]
                return [(high, parts[:, 0, cols]), (high, parts[:, 1, cols]), (low, parts[:, 0, cols]),
                        (mixed, parts[:, 2, cols]), (last_act, parts[kg, 3, cols])]

            def token_major(out_ap, *operands):
                five = passes(*operands)
                for n, (a_, w_) in enumerate(five):
                    last = pe.matmul(out_ap, a_, w_, start=(n == 0), stop=(n == len(five) - 1))
                return last

            def feature_major(out_ap, *operands):
                five = passes(*operands)
                for n, (a_, w_) in enumerate(five):
                    last = pe.matmul(out_ap, w_, a_, start=(n == 0), stop=(n == len(five) - 1))
                return last

            def half(t):
                return slice(t * T, (t + 1) * T)

            def split_transposes(bank, src):
                for t in range(2):
                    pe.transpose(bank[:, t * T:(t + 1) * T], src[:, t, 0:KA], ident_sb[0:T, 0:T])
                for t in range(2):
                    last = pe.transpose(bank[:, TOKENS + t * T:TOKENS + (t + 1) * T],
                                        src[:, t, KB:C], ident_sb[0:T, 0:T])
                return last

            def transposes(bank, src):
                for k in range(2):
                    for t in range(2):
                        last = pe.transpose(bank[0:CH, k * TOKENS + t * T:k * TOKENS + (t + 1) * T],
                                            src[:, t, k * CH:(k + 1) * CH], ident_sb[0:T, 0:T])
                return last

            def experts(x_, xp, g):
                t, pair = g % 2, g // 2
                if isinstance(x_, int) and x_ == 0 and g == 0:
                    pe.wait_ge(s_split, MADE["X"])
                if g >= 2 or old(x_, 1):
                    pe.wait_ge(ve_combined, 8 * x_ + g - 1)
                token_major(bank_x[g % 2][0:T, 0:PAIR], y1_s[xp], y1_g[xp], expert_h,
                            slice(pair * PAIR, (pair + 1) * PAIR), half(t)).then_inc(pe_expert, 1)

            def step(j, par, clip):
                a, l, b, c, x_, n, d, e, o = (clip(s) for s in "ALBCXNDEO")
                bp, cp, xp = ((par + STAGES[s]) % 2 for s in "BCX")
                if first(j, 0):
                    pe.wait_ge(s_load["front"], LOADED["front"])
                    fold_embedding()
                if first(j, 1):
                    pe.wait_ge(s_ones, 1)
                    pe.wait_ge(s_folded, 2)
                if a is not None:
                    half_count = (a // 2 + 1) * 16 if isinstance(a, int) else (a + (2 - par)) * 8
                    pe.wait_ge(s_frames[par], half_count)
                    if old(a, 1):
                        pe.wait_ge(ac_h0, a)
                    if n is not None and old(n, 1):
                        pe.wait_ge(ve_clip_var, n)
                    for t in range(2):
                        last = pe.transpose(bank_a[0:FRAME, t * T:(t + 1) * T], frame_sb[par][:, t, :],
                                            ident_sb[0:T, 0:T])
                    last.then_inc(pe_frames, 1)
                if d is not None:
                    pe.wait_ge(ac_xn, d + 1)
                    if old(d, 1):
                        pe.wait_ge(ve_probs_t, d)
                    split_transposes(bank_d, xn).then_inc(pe_y2t, 1)
                if b is not None:
                    pe.wait_ge(ac_y0, b + 1)
                    if old(b, 1):
                        pe.wait_ge(ve_h1, b)
                    transposes(bank_b, y0[bp]).then_inc(pe_y0t, 1)
                if c is not None:
                    pe.wait_ge(ve_y1, c + 1)
                    if e is not None and old(e, 1):
                        pe.wait_ge(ac_gelu, 2 * e)
                    split_transposes(bank_c, y1).then_inc(pe_y1t, 1)
                if o is not None:
                    pe.wait_ge(ac_gelu, 2 * o + 2)
                    pe.wait_ge(ac_hot_t, o + 1)
                    for t in range(2):
                        out_ap = halves(bank_e, T, C)[:, t, :]
                        for u in range(4):
                            pe.matmul(out_ap, units_h[:, u, half(t)], w2_h[:, u, :], start=(u == 0), stop=False)
                            pe.matmul(out_ap, units_h[:, u, half(t)], w2_l[:, u, :], start=False, stop=False)
                        if t == 0:
                            pe.wait_ge(po_units, 2 * o + 2)
                        for u in range(4):
                            pe.matmul(out_ap, units_l[:, u, half(t)], w2_h[:, u, :], start=False, stop=False)
                        last = pe.matmul(out_ap, hot_t[:, half(t)], b2_h[:, :], start=False, stop=True)
                    last.then_inc(pe_out, 1)
                if a is not None:
                    pe.wait_ge(ac_frame_t, a + 1)
                    pe.matmul(bank_a[0:2 * BINS, 0:TOKENS], dft_sb[:, :], frame_t[:, :],
                              start=True, stop=True).then_inc(pe_dft, 1)
                if b is not None:
                    pe.wait_ge(ac_y0t, b + 1)
                    for t in range(2):
                        for k in range(2):
                            last = pe.matmul(bank_b[0:T, t * QUERIES:(t + 1) * QUERIES],
                                             y0_t[:, k, t * T:(t + 1) * T], y0_t[:, k, 0:QUERIES],
                                             start=(k == 0), stop=(k == 1))
                    last.then_inc(pe_scores_b, 1)
                if a is not None:
                    pe.wait_ge(ac_power, a + 1)
                    pe.matmul(bank_a[0:MEL, 0:TOKENS], mel_sb[:, :], power[:, :],
                              start=True, stop=True).then_inc(pe_mel, 1)
                if d is not None:
                    if first(j, STAGES["D"]):
                        pe.wait_ge(s_split, MADE["D"])
                    pe.wait_ge(ve_xnt, d + 1)
                    for m in range(2):
                        last = feature_major(halves(bank_d, 128, TOKENS)[:, m, :], xn_s, None, qk_h,
                                             slice(m * 128, (m + 1) * 128), slice(0, TOKENS))
                    last.then_inc(pe_qk, 1)
                if c is not None:
                    if first(j, STAGES["C"]):
                        pe.wait_ge(s_split, MADE["C"])
                    pe.wait_ge(ve_y1s, c + 1)
                    for t in range(2):
                        last = token_major(bank_c[0:T, t * EXPERTS:(t + 1) * EXPERTS], y1_s[cp], y1_g[cp],
                                           router_h, slice(0, EXPERTS), half(t))
                    last.then_inc(pe_router, 1)
                if e is not None:
                    pe.wait_ge(ve_y3, e + 1)
                    if old(e, 1):
                        pe.wait_ge(ve_out, e)
                    split_transposes(bank_e, y3).then_inc(pe_y3t, 1)
                if x_ is not None:
                    experts(x_, xp, 0)
                    experts(x_, xp, 1)
                if b is not None:
                    pe.wait_ge(ac_probs_b, b + 1)
                    for t in range(2):
                        last = pe.matmul(bank_b[:, 0:C + 1], probs_b[:, t, :, :].rearrange("p r q -> p (r q)"),
                                         y0[bp][:, t, :], start=(t == 0), stop=(t == 1))
                    last.then_inc(pe_mix_b, 1)
                if d is not None:
                    pe.wait_ge(ve_qk, d + 1)
                    for t in range(2):
                        five = [(qk_th[:, 0, half(t)], xn_s[:, 0, :]), (qk_th[:, 0, half(t)], xn_s[:, 2, :]),
                                (qk_tl[:, 0, half(t)], xn_s[:, 0, :]), (qk_th[:, 1, half(t)], xn_s[:, 1, :]),
                                (qk_tl[KB:128, 1, half(t)], xn_s[KB:128, 1, :])]
                        for i, (q_, k_) in enumerate(five):
                            last = pe.matmul(halves(bank_d, T, TOKENS)[:, t, :], q_, k_,
                                             start=(i == 0), stop=(i == len(five) - 1))
                    last.then_inc(pe_scores_d, 1)
                if e is not None:
                    if first(j, STAGES["E"]):
                        pe.wait_ge(s_split, MADE["E"])
                    pe.wait_ge(ve_y3s, e + 1)
                    for t in range(2):
                        last = token_major(bank_e[0:T, t * EXPERTS:(t + 1) * EXPERTS], y3_s, y3_g,
                                           switch_h, slice(0, EXPERTS), half(t))
                    last.then_inc(pe_switch, 1)
                if l is not None:
                    if first(j, 0):
                        pe.wait_ge(s_embed, 1)
                    pe.wait_ge(ve_log, l + 1)
                    for t in range(2):
                        pe.matmul(halves(bank_a, T, C)[:, t, :], log_s[:, half(t)], embed_h[:, 0, :],
                                  start=True, stop=False)
                        last = pe.matmul(halves(bank_a, T, C)[:, t, :], log_s[0:MEL + 1, half(t)],
                                         embed_h[0:MEL + 1, 1, :], start=False, stop=True)
                    last.then_inc(pe_embed, 1)
                if x_ is not None:
                    experts(x_, xp, 2)
                if d is not None:
                    for t in range(2):
                        last = token_major(halves(bank_d2, T, C)[:, t, :], xn_s, None, wv_h,
                                           slice(0, C), half(t))
                    last.then_inc(pe_values, 1)
                if e is not None:
                    pe.wait_ge(ve_hot, e + 1)
                    for t in range(2):
                        last = pe.transpose(bank_e[0:KM, t * T:(t + 1) * T], hot[:, t, :],
                                            ident_sb[0:T, 0:T])
                    last.then_inc(pe_hot_t, 1)
                if x_ is not None:
                    experts(x_, xp, 3)
                if n is not None:
                    pe.wait_ge(ac_y2, n + 1)
                    if a is not None:
                        pe.wait_ge(ac_h0, a + 1)
                    for t in range(2):
                        last = pe.matmul(bank_a[:, 0:2], mean_w[:, :], clip_sums[:, t, :],
                                         start=(t == 0), stop=(t == 1))
                    last.then_inc(pe_clip, 1)
                if e is not None:
                    pe.wait_ge(ac_mask, e + 1)
                    if c is not None:
                        pe.wait_ge(ve_pick, c + 1)
                    for m in range(2):
                        u = m
                        last = feature_major(halves(bank_c, 128, TOKENS)[:, m, :], y3_s, y3_g, w1_h,
                                             slice(u * 128, (u + 1) * 128), slice(0, TOKENS))
                    last.then_inc(pe_hidden, 1)
                if b is not None:
                    pe.wait_ge(ve_mix_b, b + 1)
                    for n_, rows_ in enumerate((128, QUERIES + 1)):
                        last = pe.matmul(bank_b[0:QUERIES, 0:C], mix_b[0:rows_, n_, :], attn_sb[0:rows_, n_, :],
                                         start=(n_ == 0), stop=(n_ == 1))
                    last.then_inc(pe_proj_b, 1)
                if d is not None:
                    pe.wait_ge(ac_probs_d, 2 * d + 2)
                    for k in range(2):
                        for t in range(2):
                            last = pe.transpose(bank_d[0:T, k * TOKENS + t * T:k * TOKENS + (t + 1) * T],
                                                probs_d[:, t, k * T:(k + 1) * T], ident_sb[0:T, 0:T])
                    last.then_inc(pe_probs_t, 1)
                if x_ is not None:
                    experts(x_, xp, 4)
                    experts(x_, xp, 5)
                if e is not None:
                    pe.wait_ge(ac_gelu, 2 * e + 1)
                    for m in range(2):
                        u = 2 + m
                        last = feature_major(halves(bank_c, 128, TOKENS)[:, m, :], y3_s, y3_g, w1_h,
                                             slice(u * 128, (u + 1) * 128), slice(0, TOKENS))
                    last.then_inc(pe_hidden, 1)
                if d is not None:
                    pe.wait_ge(ve_probs_t, d + 1)
                    pe.wait_ge(ve_values, d + 1)
                    for t in range(2):
                        out_ap = halves(bank_d2, T, C)[:, t, :]
                        for k in range(2):
                            pe.matmul(out_ap, probs_th[:, k, half(t)], values_h[:, k, :], start=(k == 0), stop=False)
                            pe.matmul(out_ap, probs_th[:, k, half(t)], values_l[:, k, :], start=False, stop=False)
                            last = pe.matmul(out_ap, probs_tl[:, k, half(t)], values_h[:, k, :], start=False,
                                             stop=(k == 1))
                    last.then_inc(pe_mix_d, 1)
                if x_ is not None:
                    experts(x_, xp, 6)
                    experts(x_, xp, 7)
                if first(j, 0):
                    pe.wait_ge(s_embed, 1)
                    pe.wait_ge(s_load["attention"], LOADED["attention"])
                    fold_attention_and_switch()

            run(pe, step)

        @block.vector
        def _(dve):
            def low_weights(full, parts, scale, bias):
                dve.scalar_tensor_tensor(parts[:, 1, :], full[:, 0, :], scale, parts[:, 0, :],
                                         ALU.mult, ALU.subtract)
                low, high = (slice(0, BIAS_L + 1), 3) if bias else (slice(KB, 128), 2)
                last = dve.scalar_tensor_tensor(parts[low, 3, :], full[low, 1, :], scale, parts[low, high, :],
                                                ALU.mult, ALU.subtract)
                last.then_inc(s_split, 1)

            def low_parts(bank, parts):
                dve.tensor_tensor(parts[:, 2, :], bank[:, 0:TOKENS], parts[:, 0, :], ALU.subtract)
                return dve.tensor_tensor(parts[0:KB, 1, :], bank[KB:128, TOKENS:2 * TOKENS],
                                         parts[KB:128, 1, :], ALU.subtract)

            def statistics(k, src, b, own):
                for t in range(2):
                    dve.bn_stats(stats[k][:, t, :], src[:, t, :]).then_inc(ve_own, 1)
                dve.wait_ge(ve_own, own + 2)
                if old(b, 1):
                    dve.wait_ge(po_shift[k] if k in po_shift else po_rdev[k], b)
                settled(dve)
                for t in range(2):
                    last = dve.bn_aggr(moments[k][:, t, :], stats[k][:, t, :])
                last.then_inc(ve_moments[k], 1)

            def normalize(k, src, dst, b):
                dve.wait_ge(po_rdev[k], b + 1)
                for t in range(2):
                    last = dve.tensor_scalar(dst[:, t, 0:C], src[:, t, :], moments[k][:, t, 0:1],
                                             rdev[k][:, t:t + 1], ALU.subtract, ALU.mult)
                return last

            def combine(x_, xp, pair):
                so_far = h2[xp] if pair else h1[xp]
                done = 8 * x_ + 2 * pair
                if pair:
                    dve.wait_ge(ve_combined, done)
                for t in range(2):
                    dve.wait_ge(pe_expert, done + t + 1)
                    dve.scalar_tensor_tensor(h2[xp][:, t, :], bank_x[t][0:T, 0:C],
                                             mix_w[xp][:, t, 2 * pair:2 * pair + 1], so_far[:, t, :],
                                             ALU.mult, ALU.add).then_inc(ve_pair, 1)
                for t in range(2):
                    dve.wait_ge(ve_pair, done + t + 1)
                    dve.scalar_tensor_tensor(h2[xp][:, t, :], bank_x[t][0:T, C:2 * C],
                                             mix_w[xp][:, t, 2 * pair + 1:2 * pair + 2], h2[xp][:, t, :],
                                             ALU.mult, ALU.add).then_inc(ve_combined, 1)

            def step(j, par, clip):
                a, l, b, c, x_, n, d, e, o = (clip(s) for s in "ALBCXNDEO")
                lp, bp, cp, xp, dp, ep, op = ((par + STAGES[s]) % 2 for s in "LBCXDEO")
                own = own_before(j)
                if first(j, 0):
                    dve.wait_ge(s_ones, 1)
                    for g in (y1_g[0], y1_g[1], y3_g):
                        dve.memset(g[BIAS_H:BIAS_H + 1, :], 1.0)
                        dve.memset(g[BIAS_L:BIAS_L + 1, :], 1.0)
                    dve.memset(hot[:, :, BIAS_H:BIAS_H + 1], 1.0)
                    dve.memset(mask_scale[BIAS_H:BIAS_H + 1, :], 1.0)
                    dve.wait_ge(s_folded, 1)
                    dve.scalar_tensor_tensor(embed_h[0:MEL + 1, 1, :], bank_b[0:MEL + 1, 0:C], EMBED_SCALE,
                                             embed_h[0:MEL + 1, 0, :], ALU.mult, ALU.subtract).then_inc(s_embed, 1)
                if first(j, 2):
                    dve.wait_ge(s_load["attention"], LOADED["attention"])
                if d is not None:
                    dve.wait_ge(ac_xnt, d + 1)
                    low_parts(bank_d, xn_s).then_inc(ve_xnt, 1)
                if c is not None:
                    dve.wait_ge(ac_y1g, c + 1)
                    low_parts(bank_c, y1_s[cp]).then_inc(ve_y1s, 1)
                if e is not None:
                    if old(e, 1):
                        dve.wait_ge(pe_y3t, e)
                    normalize(3, h3[ep], y3, e).then_inc(ve_y3, 1)
                if o is not None:
                    dve.wait_ge(ac_route_exp, 2 * o + 2)
                    dve.tensor_scalar(route_scaled[:, :], route_sum[:, :], OUT_SCALE, None,
                                      ALU.mult).then_inc(ve_own, 1)
                    dve.wait_ge(ve_own, own + 1)
                    dve.reciprocal(route_prob[:, :], route_scaled[:, :]).then_inc(ve_own, 1)
                    own = own + 2
                    dve.wait_ge(ve_own, own)
                    dve.wait_ge(pe_out, o + 1)
                    if old(o, 2):
                        stored = (o // 2) * 16 if isinstance(o, int) else (o - op) * 8
                        dve.wait_ge(s_stored[op], stored)
                    for t in range(2):
                        last = dve.scalar_tensor_tensor(out_sb[op][:, t, :], halves(bank_e, T, C)[:, t, :],
                                                        route_prob[:, t:t + 1], h3[op][:, t, :],
                                                        ALU.mult, ALU.add)
                    last.then_inc(ve_out, 1)
                if a is not None:
                    dve.wait_ge(ac_log, a + 1)
                    dve.tensor_tensor(log_s[LOW_MEL:KE, :], log_mel[:, :], log_s[0:MEL, :],
                                      ALU.subtract).then_inc(ve_log, 1)
                if c is not None:
                    dve.wait_ge(pe_router, c + 1)
                    settled(dve)
                    for t in range(2):
                        dve.max(top[:, t, :], bank_c[0:T, t * EXPERTS:(t + 1) * EXPERTS]).then_inc(ve_own, 1)
                    dve.wait_ge(ve_own, own + 2)
                    dve.tensor_scalar(neg_top[:, :], top[:, :, 0], -1.0 / EXPERT_SCALE, None,
                                      ALU.mult).then_inc(ve_top, 1)
                    for t in range(2):
                        dve.max_index(top_at[:, t, :], top[:, t, :],
                                      bank_c[0:T, t * EXPERTS:(t + 1) * EXPERTS]).then_inc(ve_own, 1)
                    own = own + 4
                    dve.wait_ge(ve_own, own)
                    dve.tensor_tensor(pick_hot[:, :, :, :],
                                      iota_sb[0:T, :].unsqueeze(1).unsqueeze(1).to_broadcast([T, 2, 2, EXPERTS]),
                                      top_at[:, :, 0:2].unsqueeze(3).to_broadcast([T, 2, 2, EXPERTS]),
                                      ALU.is_equal).then_inc(ve_pick, 1)
                if d is not None:
                    dve.wait_ge(ac_qk, d + 1)
                    dve.tensor_tensor(qk_tl[:, :, :], halves(bank_d, 128, TOKENS), qk_th[:, :, :],
                                      ALU.subtract).then_inc(ve_qk, 1)
                if c is not None:
                    dve.wait_ge(ac_top_exp, 2 * c + 2)
                    dve.scalar_tensor_tensor(denom[:, :], exp_sum[:, :], 1e-9, top_exp[:, :, 1],
                                             ALU.mult, ALU.add).then_inc(ve_weigh, 1)
                    dve.wait_ge(ve_weigh, 5 * c + 1)
                    dve.tensor_scalar(denom1[:, :], denom[:, :], 1.0, EXPERT_SCALE, ALU.add,
                                      ALU.mult).then_inc(ve_weigh, 1)
                    dve.wait_ge(ve_weigh, 5 * c + 2)
                    dve.reciprocal(rdenom[:, :], denom1[:, :]).then_inc(ve_weigh, 1)
                    dve.wait_ge(ve_weigh, 5 * c + 3)
                    dve.tensor_tensor(pick_w[:, :, :], top_exp[:, :, 0:2],
                                      rdenom[:, :].unsqueeze(2).to_broadcast([T, 2, 2]),
                                      ALU.mult).then_inc(ve_weigh, 1)
                    dve.wait_ge(ve_weigh, 5 * c + 4)
                    dve.wait_ge(ve_pick, c + 1)
                    dve.tensor_tensor(pick_mix[:, :, :, :], pick_hot[:, :, :, :],
                                      pick_w[:, :, :].unsqueeze(3).to_broadcast([T, 2, 2, EXPERTS]),
                                      ALU.mult).then_inc(ve_weigh, 1)
                    dve.wait_ge(ve_weigh, 5 * c + 5)
                    dve.tensor_tensor(mix_w[cp][:, :, :], pick_mix[:, :, 0, :], pick_mix[:, :, 1, :],
                                      ALU.add).then_inc(ve_mix_w, 1)
                if e is not None:
                    dve.wait_ge(ac_y3g, e + 1)
                    low_parts(bank_e, y3_s).then_inc(ve_y3s, 1)
                if x_ is not None:
                    dve.wait_ge(po_h1, x_ + 1)
                    dve.wait_ge(ve_h1, x_ + 1)
                    if old(x_, 2):
                        dve.wait_ge(po_h3, x_ - 1)
                    dve.wait_ge(ve_mix_w, x_ + 1)
                    combine(x_, xp, 0)
                if d is not None:
                    dve.wait_ge(pe_scores_d, d + 1)
                    for t in range(2):
                        last = dve.tensor_reduce(neg_max[:, t:t + 1], bank_d[0:T, t * TOKENS:(t + 1) * TOKENS],
                                                 AX_X, ALU.max, negate=True)
                    last.then_inc(ve_max_d, 1)
                if e is not None:
                    dve.wait_ge(pe_switch, e + 1)
                    settled(dve)
                    for t in range(2):
                        dve.max(best[:, t, :], bank_e[0:T, t * EXPERTS:(t + 1) * EXPERTS]).then_inc(ve_own, 1)
                    dve.wait_ge(ve_own, own + 2)
                    dve.tensor_scalar(neg_best[:, :], best[:, :, 0], -1.0, None, ALU.mult).then_inc(ve_best, 1)
                    for t in range(2):
                        dve.max_index(best_at[:, t, :], best[:, t, :],
                                      bank_e[0:T, t * EXPERTS:(t + 1) * EXPERTS]).then_inc(ve_own, 1)
                    own = own + 4
                    dve.wait_ge(ve_own, own)
                    dve.tensor_tensor(hot[:, :, 0:64].rearrange("p t (i n) -> p t i n", i=2)[:, :, :, 0:EXPERTS],
                                      iota_sb[0:T, :].unsqueeze(1).unsqueeze(1).to_broadcast([T, 2, 2, EXPERTS]),
                                      best_at[:, :, 0:1].unsqueeze(3).to_broadcast([T, 2, 2, EXPERTS]),
                                      ALU.is_equal)
                    dve.tensor_tensor(hot[:, :, MASK:KM],
                                      iota_sb[0:T, :].unsqueeze(1).to_broadcast([T, 2, EXPERTS]),
                                      best_at[:, :, 0:1].to_broadcast([T, 2, EXPERTS]),
                                      ALU.not_equal).then_inc(ve_hot, 1)
                if b is not None:
                    dve.wait_ge(pe_mix_b, b + 1)
                    dve.reciprocal(rsum_b[:, :], bank_b[:, C:C + 1]).then_inc(ve_own, 1)
                    own = own + 1
                    dve.wait_ge(ve_own, own)
                    dve.tensor_scalar(mix_b[0:QUERIES, :, :],
                                      bank_b[0:QUERIES, 0:C].rearrange("q (r i) -> q i r", i=3)[:, 0:3:2, :],
                                      rsum_b[0:QUERIES, :], None, ALU.mult)
                    dve.tensor_scalar(mix_b[QUERIES:128, 0, :], bank_b[QUERIES:128, 1:C:3],
                                      rsum_b[QUERIES:128, :], None, ALU.mult).then_inc(ve_mix_b, 1)
                if l is not None:
                    dve.wait_ge(ac_h0, l + 1)
                    statistics(0, h0[lp], l, own)
                    own = own + 2
                if d is not None:
                    dve.wait_ge(ac_values, d + 1)
                    dve.scalar_tensor_tensor(values_l[:, :, :], halves(bank_d2, T, C), 1.0 / VALUE_SCALE,
                                             values_h[:, :, :], ALU.mult, ALU.subtract).then_inc(ve_values, 1)
                if x_ is not None:
                    combine(x_, xp, 1)
                if n is not None:
                    dve.wait_ge(pe_clip, n + 1)
                    if old(n, 1):
                        dve.wait_ge(po_clip_rdev, n)
                    dve.tensor_copy(clip_moments[:, :], bank_a[:, 0:2]).then_inc(ve_own, 1)
                    dve.wait_ge(ve_own, own + 1)
                    dve.tensor_tensor(mean_sq[:, :], clip_moments[:, 0:1], clip_moments[:, 0:1],
                                      ALU.mult).then_inc(ve_own, 1)
                    dve.wait_ge(ve_own, own + 2)
                    dve.tensor_tensor(clip_var[:, :], clip_moments[:, 1:2], mean_sq[:, :],
                                      ALU.subtract).then_inc(ve_clip_var, 1)
                    own = own + 2
                if b is not None:
                    dve.wait_ge(pe_proj_b, b + 1)
                    dve.wait_ge(po_h1, b + 1)
                    dve.tensor_tensor(h1[bp][0:QUERIES, 0, :], bank_b[0:QUERIES, 0:C], h0[bp][0:QUERIES, 0, :],
                                      ALU.add).then_inc(ve_h1, 1)
                    dve.wait_ge(ve_h1, b + 1)
                    statistics(1, h1[bp], b, own)
                    own = own + 2
                if d is not None:
                    dve.wait_ge(ac_probs_t, d + 1)
                    dve.tensor_tensor(probs_tl[:, :, :], halves(bank_d, T, TOKENS), probs_th[:, :, :],
                                      ALU.subtract).then_inc(ve_probs_t, 1)
                if x_ is not None:
                    combine(x_, xp, 2)
                if b is not None:
                    if old(b, 1):
                        dve.wait_ge(pe_y1t, b)
                    normalize(1, h1[bp], y1, b).then_inc(ve_y1, 1)
                if d is not None:
                    dve.wait_ge(ac_probs_d, 2 * d + 2)
                    dve.reciprocal(rsum_d[:, :], sum_d[:, :]).then_inc(ve_own, 1)
                    own = own + 1
                    dve.wait_ge(ve_own, own)
                    dve.wait_ge(pe_mix_d, d + 1)
                    dve.wait_ge(po_h3, d + 1)
                    for t in range(2):
                        last = dve.scalar_tensor_tensor(h3[dp][:, t, :], halves(bank_d2, T, C)[:, t, :],
                                                        rsum_d[:, t:t + 1], h3[dp][:, t, :],
                                                        ALU.mult, ALU.add)
                    last.then_inc(ve_h3, 1)
                    dve.wait_ge(ve_h3, d + 1)
                    statistics(3, h3[dp], d, own)
                    own = own + 2
                if x_ is not None:
                    combine(x_, xp, 3)
                    dve.wait_ge(ve_combined, 8 * x_ + 8)
                    statistics(2, h2[xp], x_, own)
                    own = own + 2
                if isinstance(j, int) and j in SPLITS:
                    for n_, (full, parts, scale, bias, _) in enumerate(SPLITS[j]):
                        dve.wait_ge(s_high, sum(len(SPLITS[i]) for i in SPLITS if i < j) + n_ + 1)
                        low_weights(full, parts, scale, bias)
                if first(j, OUT_WEIGHTS):
                    dve.wait_ge(s_high, 7)
                    dve.scalar_tensor_tensor(w2_l[:, :, :], w2_sb[:, :, :], OUT_SCALE, w2_h[:, :, :],
                                             ALU.mult, ALU.subtract)
                    dve.scalar_tensor_tensor(b2_h[32:KB2, :], b2_f[32:KB2, :], OUT_SCALE, b2_h[32:KB2, :],
                                             ALU.mult, ALU.subtract).then_inc(s_split, 1)

            OWN = {"L": 2, "B": 1 + 2, "C": 4, "X": 2, "N": 2, "D": 1 + 2, "E": 4, "O": 2}

            def own_before(j):
                return before(OWN, j)

            run(dve, step)


def kernel(**inputs):
    import numpy as np
    import concourse.bacc as bacc
    from concourse.bass_utils import run_bass_kernel_spmd

    def rows(*parts):
        return np.concatenate([np.atleast_2d(p) for p in parts], axis=0)

    def with_bias(w, bias):
        between = np.zeros((BIAS_H - BIAS_L - 1, w.shape[1]), np.float32)
        return rows(w, bias, between, bias)

    given = {k: np.asarray(v) for k, v in inputs.items()}
    n = np.arange(FRAME)
    window = (0.54 - 0.46 * np.cos(2.0 * np.pi * n / (FRAME - 1))).astype(np.float32).astype(np.float64)
    angle = 2.0 * np.pi * ((n[:, None] * np.arange(BINS)[None, :]) % FRAME) / FRAME
    dft = np.concatenate([window[:, None] * np.cos(angle), -window[:, None] * np.sin(angle)], axis=1)
    one_hot_row = np.zeros((1, MEL + 1), np.float32)
    one_hot_row[0, MEL] = 1.0
    enc_row = np.zeros((1, C + 1), np.float32)
    enc_row[0, C] = 1.0
    g = given
    arrays = {
        "x": g["x"],
        "dft": dft.astype(np.float32),
        "ident": np.eye(128, dtype=np.float32),
        "iota": np.tile(np.arange(EXPERTS, dtype=np.float32), (128, 1)),
        "mel_w": rows(g["L0_tok_mel_filters"].T, g["L0_tok_mel_filters"].T),
        "dct_w": rows(np.concatenate([g["L0_tok_dct"], np.zeros((MFCC, 1), np.float32)], axis=1), one_hot_row),
        "embed_w": rows(g["L0_tok_w_proj"], g["L0_tok_b_proj"]),
        "attn_w": rows(g["L0_attn_proj_w"].T, g["L0_attn_proj_b"]),
        "router_w": with_bias(g["L0_ffn_router_w"].T, g["L0_ffn_router_b"]),
        "expert_w": with_bias(g["L0_ffn_expert_w"].transpose(2, 0, 1).reshape(C, EXPERTS * C),
                              g["L0_ffn_expert_b"].reshape(1, EXPERTS * C)),
        "wq": g["L1_attn_Wq"],
        "wk": g["L1_attn_Wk"],
        "wv": rows(g["L1_attn_Wv"].T, g["L1_attn_Wv"].T[KA:]),
        "enc_w": rows(np.concatenate([g["L1_ffn_enc_w"].T, g["L1_ffn_enc_b"][:, None]], axis=1), enc_row),
        "switch_w": rows(g["L1_ffn_sw_w"], g["L1_ffn_sw_b"]),
        "w1": rows(with_bias(g["L1_ffn_w1"].transpose(1, 0, 2).reshape(C, EXPERTS * HID),
                             g["L1_ffn_b1"].reshape(1, EXPERTS * HID)),
                   np.repeat(np.eye(EXPERTS, dtype=np.float32) * -(MASK_W / HIDDEN_SCALE), HID, axis=1)),
        "w2": g["L1_ffn_w2"].reshape(EXPERTS * HID, C),
        "b2": rows(g["L1_ffn_b2"], np.zeros((32 - EXPERTS, C), np.float32), g["L1_ffn_b2"]),
    }
    arrays = {f"in_{k}": np.ascontiguousarray(v) for k, v in arrays.items()}
    nc = bacc.Bacc("TRN2", target_bir_lowering=False, num_devices=1)
    args = [nc.dram_tensor(k, v.shape, mybir.dt.from_np(v.dtype), kind="ExternalInput").ap()
            for k, v in arrays.items()]
    out = nc.dram_tensor("out_0", (CLIPS, TOKENS, C), F32, kind="ExternalOutput").ap()
    tower(nc, *args, out)
    result = run_bass_kernel_spmd(nc, [arrays], core_ids=[0])
    return result.results[0]["out_0"]
```
